# Optimizing a Trainium2 kernel written in Bass

```python
import numpy as np
import jax
import jax.numpy as jnp

def _softmax(x, axis=-1):
    return jax.nn.softmax(x, axis=axis)

def _gelu(x):
    return jax.nn.gelu(x, approximate=True)

def _silu(x):
    return jax.nn.silu(x)

def _sigmoid(x):
    return jax.nn.sigmoid(x)

def _layernorm(x, axis=-1, eps=1e-05):
    m = jnp.mean(x, axis=axis, keepdims=True)
    v = jnp.var(x, axis=axis, keepdims=True)
    return (x - m) / jnp.sqrt(v + eps)

def _scatter_add(tgt, idx, src, axis=0):
    return tgt.at[idx].add(src)

def _segment_sum(src, seg, n):
    return jax.ops.segment_sum(src, seg, n)
kernel_name = 'mk_early_fusion_d1_tok_img768_r4_d892bf'

def setup_inputs(seed: int=0):
    np.random.seed(seed)
    _w = jnp.asarray

    def _rec_inputs():
        import jax
        import jax.numpy as jnp
        _rk = jax.random.key(seed)
        x = -0.000147625 + 0.999875 * jax.random.normal(jax.random.fold_in(_rk, 1), (32, 3, 224, 224), jnp.float32)
        txt = 0.000690276 + 0.553291 * jax.random.normal(jax.random.fold_in(_rk, 2), (32, 77, 192), jnp.float32)
        return (x, txt)
    x, txt = _rec_inputs()

    def _L0_tok_setup():
        import jax, jax.numpy as jnp
        import numpy as np
        PATCH = 16
        key = jax.random.key(seed)
        ks = jax.random.split(key, 5)
        B, C, H, W = (64, 3, 224, 224)
        D = 192
        NP = H // PATCH * (W // PATCH)
        return {'x': jax.random.normal(ks[0], (B, C, H, W), jnp.float32), 'conv_w': jax.random.normal(ks[1], (D, C, PATCH, PATCH), jnp.float32) * 0.02, 'conv_b': jax.random.normal(ks[2], (D,), jnp.float32) * 0.02, 'cls_token': jax.random.normal(ks[3], (1, 1, D), jnp.float32) * 0.02, 'pos_emb': jax.random.normal(ks[4], (1, NP + 1, D), jnp.float32) * 0.02}
    _L0_tok_all = _L0_tok_setup()
    _L0_tok_in = {k: v for k, v in _L0_tok_all.items() if k in ('conv_w', 'conv_b', 'cls_token', 'pos_emb')}
    del _L0_tok_all

    def _L0_attn_setup():
        import jax, jax.numpy as jnp
        import numpy as np
        D_MODEL, D_STATE, D_INNER, DT_RANK, D_CONV, K = (192, 16, 384, 48, 3, 2)
        B_SZ, L_SEQ = (2, 512)

        def _selective_scan(u, delta, A, Bp, Cp, Dk):

            def step(h, inp):
                d_t, u_t, b_t, c_t = inp
                dA = jnp.exp(d_t[..., None] * A)
                h = h * dA + (d_t * u_t)[..., None] * b_t[:, None, :]
                y_t = jnp.einsum('bdn,bn->bd', h, c_t)
                return (h, y_t)
            h0 = jnp.zeros((u.shape[0], u.shape[2], A.shape[1]), dtype=u.dtype)
            xs = (jnp.swapaxes(delta, 0, 1), jnp.swapaxes(u, 0, 1), jnp.swapaxes(Bp, 0, 1), jnp.swapaxes(Cp, 0, 1))
            _, ys = jax.lax.scan(step, h0, xs)
            return jnp.swapaxes(ys, 0, 1) + u * Dk

        def _direction(u_k, xw_k, dtw_k, dtb_k, Alog_k, D_k):
            x_dbl = jnp.einsum('bld,rd->blr', u_k, xw_k)
            dt_in, Bp, Cp = jnp.split(x_dbl, [DT_RANK, DT_RANK + D_STATE], axis=-1)
            delta = jax.nn.softplus(jnp.einsum('blr,dr->bld', dt_in, dtw_k) + dtb_k)
            A = -jnp.exp(Alog_k)
            return _selective_scan(u_k, delta, A, Bp, Cp, D_k)
        key = jax.random.key(seed)
        ks = jax.random.split(key, 10)
        s = lambda k, shp, sc=0.02: jax.random.normal(k, shp, dtype=jnp.float32) * sc
        return {'x': jax.random.normal(ks[0], (B_SZ, L_SEQ, D_MODEL), dtype=jnp.float32), 'in_proj_w': s(ks[1], (2 * D_INNER, D_MODEL)), 'conv_w': s(ks[2], (D_INNER, 1, D_CONV), 0.3), 'conv_b': s(ks[3], (D_INNER,), 0.1), 'x_proj_w': s(ks[4], (K, DT_RANK + 2 * D_STATE, D_INNER)), 'dt_proj_w': s(ks[5], (K, D_INNER, DT_RANK), 0.1), 'dt_proj_b': s(ks[6], (K, D_INNER), 0.1), 'A_logs': s(ks[7], (K * D_INNER, D_STATE), 0.5), 'Ds': jnp.ones((K * D_INNER,), dtype=jnp.float32), 'out_proj_w': s(ks[8], (D_MODEL, D_INNER))}
    _L0_attn_all = _L0_attn_setup()
    _L0_attn_in = {k: v for k, v in _L0_attn_all.items() if k in ('in_proj_w', 'conv_w', 'conv_b', 'x_proj_w', 'dt_proj_w', 'dt_proj_b', 'A_logs', 'Ds', 'out_proj_w')}
    del _L0_attn_all

    def _L0_ffn_setup():
        import jax, jax.numpy as jnp
        import numpy as np
        S, B, DIM = (256, 4, 192)
        N_EXPERTS = 8
        HID = 512
        key = jax.random.key(seed)
        ks = jax.random.split(key, 6)
        scale = 0.02
        return {'hidden_states': jax.random.normal(ks[0], (S, B, DIM), dtype=jnp.float32), 'router_w': jax.random.normal(ks[1], (DIM, N_EXPERTS), dtype=jnp.float32) * scale, 'router_b': jnp.zeros((N_EXPERTS,), dtype=jnp.float32), 'w1': jax.random.normal(ks[2], (N_EXPERTS, DIM, HID), dtype=jnp.float32) * scale, 'w2': jax.random.normal(ks[3], (N_EXPERTS, DIM, HID), dtype=jnp.float32) * scale, 'w3': jax.random.normal(ks[4], (N_EXPERTS, HID, DIM), dtype=jnp.float32) * scale}
    _L0_ffn_all = _L0_ffn_setup()
    _L0_ffn_in = {k: v for k, v in _L0_ffn_all.items() if k in ('router_w', 'router_b', 'w1', 'w2', 'w3')}
    del _L0_ffn_all
    return {'x': x, 'txt': txt, 'L0_tok_conv_w': _L0_tok_in['conv_w'], 'L0_tok_conv_b': _L0_tok_in['conv_b'], 'L0_tok_cls_token': _L0_tok_in['cls_token'], 'L0_tok_pos_emb': _L0_tok_in['pos_emb'], 'L0_attn_in_proj_w': _L0_attn_in['in_proj_w'], 'L0_attn_conv_w': _L0_attn_in['conv_w'], 'L0_attn_conv_b': _L0_attn_in['conv_b'], 'L0_attn_x_proj_w': _L0_attn_in['x_proj_w'], 'L0_attn_dt_proj_w': _L0_attn_in['dt_proj_w'], 'L0_attn_dt_proj_b': _L0_attn_in['dt_proj_b'], 'L0_attn_A_logs': _L0_attn_in['A_logs'], 'L0_attn_Ds': _L0_attn_in['Ds'], 'L0_attn_out_proj_w': _L0_attn_in['out_proj_w'], 'L0_ffn_router_w': _L0_ffn_in['router_w'], 'L0_ffn_router_b': _L0_ffn_in['router_b'], 'L0_ffn_w1': _L0_ffn_in['w1'], 'L0_ffn_w2': _L0_ffn_in['w2'], 'L0_ffn_w3': _L0_ffn_in['w3']}

def reference(x, txt, L0_tok_conv_w, L0_tok_conv_b, L0_tok_cls_token, L0_tok_pos_emb, L0_attn_in_proj_w, L0_attn_conv_w, L0_attn_conv_b, L0_attn_x_proj_w, L0_attn_dt_proj_w, L0_attn_dt_proj_b, L0_attn_A_logs, L0_attn_Ds, L0_attn_out_proj_w, L0_ffn_router_w, L0_ffn_router_b, L0_ffn_w1, L0_ffn_w2, L0_ffn_w3):
    import jax
    import jax.numpy as jnp

    def _L0_tok_ref(x, conv_w, conv_b, cls_token, pos_emb):
        import jax, jax.numpy as jnp
        import numpy as np
        PATCH = 16
        B, C, H, W = x.shape
        D = conv_w.shape[0]
        nh, nw = (H // PATCH, W // PATCH)
        patches = x.reshape(B, C, nh, PATCH, nw, PATCH).transpose(0, 2, 4, 1, 3, 5)
        patches = patches.reshape(B, nh * nw, C * PATCH * PATCH)
        w = conv_w.reshape(D, C * PATCH * PATCH)
        tokens = jnp.einsum('bnk,dk->bnd', patches, w) + conv_b
        cls = jnp.broadcast_to(cls_token, (B, 1, D))
        out = jnp.concatenate([cls, tokens], axis=1)
        return out + pos_emb

    def _L0_attn_ref(x, in_proj_w, conv_w, conv_b, x_proj_w, dt_proj_w, dt_proj_b, A_logs, Ds, out_proj_w):
        import jax, jax.numpy as jnp
        import numpy as np
        D_MODEL, D_STATE, D_INNER, DT_RANK, D_CONV, K = (192, 16, 384, 48, 3, 2)
        B_SZ, L_SEQ = (2, 512)

        def _selective_scan(u, delta, A, Bp, Cp, Dk):

            def step(h, inp):
                d_t, u_t, b_t, c_t = inp
                dA = jnp.exp(d_t[..., None] * A)
                h = h * dA + (d_t * u_t)[..., None] * b_t[:, None, :]
                y_t = jnp.einsum('bdn,bn->bd', h, c_t)
                return (h, y_t)
            h0 = jnp.zeros((u.shape[0], u.shape[2], A.shape[1]), dtype=u.dtype)
            xs = (jnp.swapaxes(delta, 0, 1), jnp.swapaxes(u, 0, 1), jnp.swapaxes(Bp, 0, 1), jnp.swapaxes(Cp, 0, 1))
            _, ys = jax.lax.scan(step, h0, xs)
            return jnp.swapaxes(ys, 0, 1) + u * Dk

        def _direction(u_k, xw_k, dtw_k, dtb_k, Alog_k, D_k):
            x_dbl = jnp.einsum('bld,rd->blr', u_k, xw_k)
            dt_in, Bp, Cp = jnp.split(x_dbl, [DT_RANK, DT_RANK + D_STATE], axis=-1)
            delta = jax.nn.softplus(jnp.einsum('blr,dr->bld', dt_in, dtw_k) + dtb_k)
            A = -jnp.exp(Alog_k)
            return _selective_scan(u_k, delta, A, Bp, Cp, D_k)
        xz = x @ in_proj_w.T
        x_conv, z = jnp.split(xz, 2, axis=-1)
        xc = jnp.swapaxes(x_conv, 1, 2)
        pad = (D_CONV - 1) // 2
        xc = jax.lax.conv_general_dilated(xc, conv_w, window_strides=(1,), padding=[(pad, pad)], feature_group_count=D_INNER, dimension_numbers=('NCH', 'OIH', 'NCH'))
        xc = xc + conv_b[None, :, None]
        u = jnp.swapaxes(jax.nn.silu(xc), 1, 2)
        u_dirs = jnp.stack([u, jnp.flip(u, axis=1)])
        A_logs_k = A_logs.reshape(K, D_INNER, D_STATE)
        Ds_k = Ds.reshape(K, D_INNER)
        y_dirs = jax.vmap(_direction)(u_dirs, x_proj_w, dt_proj_w, dt_proj_b, A_logs_k, Ds_k)
        y_scanned = y_dirs[0] + jnp.flip(y_dirs[1], axis=1)
        y_gated = y_scanned * z
        return y_gated @ out_proj_w.T

    def _L0_ffn_ref(hidden_states, router_w, router_b, w1, w2, w3):
        import jax, jax.numpy as jnp
        import numpy as np
        S, B, DIM = (256, 4, 192)
        N_EXPERTS = 8
        HID = 512
        s, b, h = hidden_states.shape
        route = jax.nn.softmax(hidden_states @ router_w + router_b, axis=2)
        max_prob = jnp.max(route, axis=2).reshape(-1, 1)
        max_ind = jnp.argmax(route, axis=2).reshape(-1)
        x = hidden_states.reshape(-1, h)
        out = jnp.zeros_like(x)
        for e in range(N_EXPERTS):
            mask = (max_ind == e)[:, None]
            xe = jnp.where(mask, x, 0.0)
            oe = jax.nn.silu(xe @ w1[e]) * (xe @ w2[e]) @ w3[e]
            out = out + jnp.where(mask, oe, 0.0)
        out = out.astype(jnp.bfloat16) * max_prob
        return out.reshape(s, b, h)
    h = _L0_tok_ref(x, L0_tok_conv_w, L0_tok_conv_b, L0_tok_cls_token, L0_tok_pos_emb)
    h = jnp.concatenate([h, txt], axis=1)
    h = h + _L0_attn_ref(_layernorm(h, axis=-1), L0_attn_in_proj_w, L0_attn_conv_w, L0_attn_conv_b, L0_attn_x_proj_w, L0_attn_dt_proj_w, L0_attn_dt_proj_b, L0_attn_A_logs, L0_attn_Ds, L0_attn_out_proj_w)
    h = h + _L0_ffn_ref(_layernorm(h, axis=-1), L0_ffn_router_w, L0_ffn_router_b, L0_ffn_w1, L0_ffn_w2, L0_ffn_w3)
    return h

_drawn_inputs = setup_inputs


def setup_inputs(seed=0):
    import zlib

    import numpy as np

    out = dict(_drawn_inputs(seed))
    spreads = {'L0_attn_Ds': (1.0, 0.6), 'L0_ffn_router_b': (0.0, 0.8)}
    factors = {'L0_tok_cls_token': 8.0,
     'L0_attn_conv_b': 3.088,
     'L0_attn_x_proj_w': 8.0,
     'L0_attn_dt_proj_w': 8.0,
     'L0_attn_dt_proj_b': 8.0,
     'L0_attn_A_logs': 8.0,
     'L0_ffn_router_w': 8.0,
     'L0_ffn_w1': 8.0,
     'L0_ffn_w2': 8.0,
     'L0_ffn_w3': 8.0}
    for name, (base, spread) in spreads.items():
        noise = np.random.default_rng([zlib.crc32(name.encode()), seed]).standard_normal(out[name].shape)
        drawn = base * np.exp(spread * noise) if base else spread * noise
        out[name] = jnp.asarray(drawn.astype(out[name].dtype))
    for name, factor in factors.items():
        out[name] = (out[name] * factor).astype(out[name].dtype)
    return out
```

```python
import concourse.bass as bass
from concourse import mybir
from contextlib import ExitStack


def early_fusion_kernel(nc: bass.Bass, patches, txt, convT, conv_bias, cls, pos, inT, dw_w, dw_b, xpT, dtT, dt_b,
                        a_logs, d_skip, outT, router_w, router_b, w1, w2, w3, out):
    f32, bf16, u32, i32 = mybir.dt.float32, mybir.dt.bfloat16, mybir.dt.uint32, mybir.dt.int32
    ALU, ACT, AX = mybir.AluOpType, mybir.ActivationFunctionType, mybir.AxisListType

    B = patches.shape[0]
    KC = patches.shape[2]
    NPOS = patches.shape[3]
    NTXT = txt.shape[1]
    D = txt.shape[2]
    DH = D // 2
    L = NPOS + NTXT
    J = outT.shape[1]
    NS = a_logs.shape[2]
    RANK = (dtT.shape[0] - 64) if dtT.shape[0] > 64 else dtT.shape[0]
    E = router_w.shape[2]
    HID = w1.shape[3]
    HC = HID // 128
    T = B * L
    EPS = 1e-5
    ROWS = [(NPOS + 1) // 2, NPOS // 2, NTXT]
    OFF = [0, ROWS[0], NPOS]
    R0 = ROWS[0]

    NT = (T + 127) // 128
    NX = (NT * 128 - E) // 128 + E
    hn_d = nc.dram_tensor("ln1_T", (B, DH, 2 * L), f32, kind="Internal").ap()
    h0_d = nc.dram_tensor("h0", (B, R0, 3 * D), f32, kind="Internal").ap()
    h1_d = nc.dram_tensor("h1", (NT * 128, D), f32, kind="Internal").ap()
    sorted_x = nc.dram_tensor("sorted_x", (NX * 128, D), f32, kind="Internal").ap()
    sorted_y = nc.dram_tensor("sorted_y", (NX * 128, D), bf16, kind="Internal").ap()

    top = ExitStack()
    with top:
        def sem(name):
            return top.enter_context(nc.semaphore(name))

        def sb(stack, name, shape, dt=f32):
            return stack.enter_context(nc.sbuf_tensor(name, shape, dt))

        def ps(stack, name, shape):
            return stack.enter_context(nc.psum_tensor(name, shape, f32))

        ident = sb(top, "ident", [128, 128])
        zero_s = sb(top, "zero_s", [128, D])

        s1 = ExitStack()
        convT_s = sb(s1, "convT_s", [128, KC, D])
        posb = sb(s1, "posb", [R0, 2, D])
        emb_bias = sb(s1, "emb_bias", [R0, 2, D])
        xt = [sb(s1, f"xt{p}", [128, KC, NPOS]) for p in range(2)]
        h0 = [sb(s1, f"h0_{p}", [R0, 3, D]) for p in range(2)]
        xn = [sb(s1, f"xn{p}", [R0, 3, D]) for p in range(2)]
        hnT = [sb(s1, f"hnT{p}", [DH, 2, L]) for p in range(2)]
        bst = [sb(s1, f"bst{p}", [R0, 3, 6]) for p in range(2)]
        sd = [sb(s1, f"sd{p}", [R0, 6, 3]) for p in range(2)]
        rt = [sb(s1, f"rt{p}", [R0, 3]) for p in range(2)]
        ps1 = ExitStack()
        emb_ps = ps(ps1, "emb_ps", [128, 2, 2, 512])
        tr_ps = ps(ps1, "tr_ps", [128, 2, 2, 512])
        s1.close()
        ps1.close()

        HN = NS // 2
        PAIRS = HN // 2
        RING = 6
        s2 = ExitStack()
        inT_s = sb(s2, "inT_s", [DH, 2, 2 * J * 128])
        xpT_s = sb(s2, "xpT_s", [128, J, xpT.shape[2]])
        dtT_s = sb(s2, "dtT_s", [dtT.shape[0], J * 128])
        outT_s = sb(s2, "outT_s", [128, J, D])
        dww = sb(s2, "dww", [128, J, 3])
        dwb = sb(s2, "dwb", [128, J])
        dtb = sb(s2, "dtb", [128, 2 * J])
        alog = sb(s2, "alog", [128, 2 * J, NS])
        a_neg = sb(s2, "a_neg", [128, 2 * J, NS])
        dsk = sb(s2, "dsk", [128, 2 * J])
        dsum = sb(s2, "dsum", [128, J])
        diag_d = sb(s2, "diag_d", [128, J, 128])
        sel = sb(s2, "sel", [96, 2 * NS, 128], bf16)
        hx = [sb(s2, f"hx{p}", [DH, 2, L]) for p in range(2)]
        hres = [sb(s2, f"hres{p}", [R0, 3, D]) for p in range(2)]
        xc = sb(s2, "xc", [128, J, L])
        u_s = sb(s2, "u_s", [128, J, L])
        z_s = [sb(s2, f"z_s{p}", [128, J, L]) for p in range(2)]
        dt_in = sb(s2, "dt_in", [dtT.shape[0], L])
        bcf = sb(s2, "bcf", [96, 2, L])
        rest1 = sb(s2, "rest1", [96, L])
        mid = sb(s2, "mid", [96, L], bf16)
        bcs = [sb(s2, f"bcs{p}", [96, 2, L], bf16) for p in range(2)]
        absx = sb(s2, "absx", [128, J, L])
        relx = sb(s2, "relx", [128, J, L])
        delta = sb(s2, "delta", [128, 2, J, L])
        du = [sb(s2, f"du{p}", [128, 2, J, L]) for p in range(2)]
        dA = [sb(s2, f"dA{v}", [128, J, HN, L + 1]) for v in range(2)]
        h_s = sb(s2, "h_s", [128, J, HN, L + 1])
        hc = sb(s2, "hc", [128, RING, 2, L])
        yg = sb(s2, "yg", [128, J, L])
        ps2 = ExitStack()
        bc_ps = ps(ps2, "bc_ps", [128, 2, 2, 512])
        y_ps = ps(ps2, "y_ps", [128, J, 512])
        misc = ps(ps2, "misc", [128, 512])
        s2.close()
        ps2.close()

        s3 = ExitStack()
        w1_s = sb(s3, "w1_s", [DH, 2, E, HID])
        w2_s = sb(s3, "w2_s", [DH, 2, E, HID])
        w3_s = sb(s3, "w3_s", [128, HC, E, D])
        xn2 = sb(s3, "xn2", [128, NT, D])
        bst2 = sb(s3, "bst2", [128, NT, 6])
        stat = sb(s3, "stat", [128, 6, NT])
        root = sb(s3, "root", [128, NT])
        rw_s = sb(s3, "rw_s", [DH, 2, E])
        rb_s = sb(s3, "rb_s", [128, E])
        x2T = [sb(s3, f"x2T{p}", [DH, 2, 128]) for p in range(2)]
        lg = sb(s3, "lg", [128, NT, E])
        lt = sb(s3, "lt", [128, NT, E])
        lmax = sb(s3, "lmax", [128, NT])
        best = sb(s3, "best", [128, NT])
        prob = sb(s3, "prob", [128, NT])
        onehot = sb(s3, "onehot", [128, NT, E])
        tri = sb(s3, "tri", [128, 128])
        ones = sb(s3, "ones", [128, 128])
        rank_e = sb(s3, "rank_e", [128, NT, E])
        cnt = sb(s3, "cnt", [128, E, NT])
        cum = sb(s3, "cum", [128, E, NT + 1])
        tot_i = sb(s3, "tot_i", [128, E], i32)
        pad_f = sb(s3, "pad_f", [128, E])
        ends = sb(s3, "ends", [128, E + 1])
        prio = sb(s3, "prio", [128, E])
        slot_f = sb(s3, "slot_f", [128, NT])
        slot_u = sb(s3, "slot_u", [128, NT], u32)
        start_f = sb(s3, "start_f", [1, NX])
        texp = sb(s3, "texp", [1, NX])
        texp_i = sb(s3, "texp_i", [1, NX], i32)
        xs = [sb(s3, f"xs{p}", [128, D]) for p in range(2)]
        xsT = [sb(s3, f"xsT{p}", [DH, 2, 128]) for p in range(2)]
        g1 = [sb(s3, f"g1_{p}", [128, HID]) for p in range(2)]
        act_s = [sb(s3, f"act_s{p}", [128, HID]) for p in range(2)]
        actT = [sb(s3, f"actT{p}", [128, HC, 128]) for p in range(2)]
        ys = [sb(s3, f"ys{p}", [128, D], bf16) for p in range(2)]
        yr = sb(s3, "yr", [128, NT, D], bf16)
        s3.close()
        ps3 = ExitStack()
        tr3 = ps(ps3, "tr3", [128, 2, 512])
        up_ps = ps(ps3, "up_ps", [128, 2, 2, 512])
        at_ps = ps(ps3, "at_ps", [128, 512])
        dn_ps = ps(ps3, "dn_ps", [128, 512])
        ps3.close()
        TB = 512 // E
        NB = (NT + TB - 1) // TB
        lg_ps = up_ps[:, 0, :, :]
        cnt_ps = [at_ps, dn_ps]
        assert NB <= 2 and NT <= 128

        w1_in = sem("w1_in")
        w2_in = sem("w2_in")
        w3_in = sem("w3_in")
        gp_set = sem("gp_set")
        clear1 = sem("clear1")
        posb_ok = sem("posb_ok")
        xt_in = [sem(f"xt_in{p}") for p in range(2)]
        txt_in = [sem(f"txt_in{p}") for p in range(2)]
        emb_mm = sem("emb_mm")
        h0_ok = sem("h0_ok")
        st_chain = sem("st_chain")
        sqrt_ok = sem("sqrt_ok")
        xn_ok = sem("xn_ok")
        tr_ok = sem("tr_ok")
        hnT_ok = sem("hnT_ok")
        hn_out = [sem(f"hn_out{p}") for p in range(2)]
        h0_out = [sem(f"h0_out{p}") for p in range(2)]

        set2 = sem("set2")
        pads = sem("pads")
        hx_in = [sem(f"hx_in{p}") for p in range(2)]
        hres_in = [sem(f"hres_in{p}") for p in range(2)]
        misc_full = sem("misc_full")
        misc_free = sem("misc_free")
        xc_mid = sem("xc_mid")
        xc_left = sem("xc_left")
        u_ok = sem("u_ok")
        sp_exp = sem("sp_exp")
        sp_ln = sem("sp_ln")
        bcf_ok = sem("bcf_ok")
        split = sem("split")
        delta_ok = sem("delta_ok")
        du_ok = sem("du_ok")
        bc_full = sem("bc_full")
        dbu = sem("dbu")
        da_ok = sem("da_ok")
        scan_ok = sem("scan_ok")
        hc_full = sem("hc_full")
        hc_free = sem("hc_free")
        skip_ok = sem("skip_ok")
        gated = sem("gated")
        h1_out = [sem(f"h1_out{p}") for p in range(2)]

        zero_ok = sem("zero_ok")
        zero_out = sem("zero_out")
        H1_PARTS = [(0, NT // 4), (NT // 4, NT // 2), (NT // 2, NT)]
        h1_in = [sem(f"h1_in{n}") for n in range(len(H1_PARTS))]
        wr_in = sem("wr_in")
        ln2 = sem("ln2")
        sqrt2 = sem("sqrt2")
        xn2_ok = sem("xn2_ok")
        tr2_ok = sem("tr2_ok")
        x2T_ok = sem("x2T_ok")
        lg_ok = sem("lg_ok")
        route = sem("route")
        rexp = sem("rexp")
        rank_ok = sem("rank_ok")
        scat = sem("scat")
        xs_in = [sem(f"xs_in{p}") for p in range(2)]
        xsT_ps = sem("xsT_ps")
        xsT_ok = sem("xsT_ok")
        up_ok = sem("up_ok")
        g1_ok = sem("g1_ok")
        act_ok = sem("act_ok")
        actT_ps = sem("actT_ps")
        actT_ok = sem("actT_ok")
        dn_ok = sem("dn_ok")
        ys_ok = sem("ys_ok")
        ys_out = [sem(f"ys_out{p}") for p in range(2)]
        h1_back = sem("h1_back")
        yr_in = sem("yr_in")
        fin_ok = sem("fin_ok")
        fin_out = sem("fin_out")

        LN2_VAR = NT + 7
        PADDED = NT * 128 > T
        GROUP = 8
        W1_DMAS = 6
        W2_DMAS = 9
        W3_DMAS = 3
        ROUTE_LT = NB + 3
        ROUTE_HOT = NB + 5
        ROUTE_ALL = ROUTE_HOT + 2 + 2 * NB + 1 + E + 3 + 2 + 5 + E + 1

        block = top.enter_context(nc.Block())

        USES = [(0, 3, "o", 0, 0), (0, 3, "o", 1, 0), (0, 3, "o", 2, 0),
                (1, 2, "z", 0, 0), (1, 3, "z", 1, 0), (1, 3, "z", 2, 0),
                (1, 3, "x", 0, 0), (1, 3, "x", 1, 0), (1, 3, "x", 2, 0),
                (2, 2, "dt", 0, 0), (2, 3, "bc", 0, 0), (2, 3, "bc", 0, 1),
                (2, 3, "p", 0, 0), (2, 3, "p", 1, 0), (2, 3, "p", 2, 0),
                (3, 3, "p", 0, 1), (3, 3, "p", 1, 1), (3, 3, "p", 2, 1)]
        SUMS = [(5, 3), (6, 2), (7, 2), (8, 2), (9, 2), (10, 1)]
        NO = 3
        NF = len(USES) - NO

        def use_count(i, n):
            if isinstance(i, int) and i == B:
                return use_count(B - 1, NO) + n
            return n - NO if i is None else NF + len(USES) * i - NO + n

        LAST_USES = use_count(B - 1, NO)

        def uses_at(i, unit, step):
            found = []
            for n, (a, b, kind, j, k) in enumerate(USES):
                if (a, b) == (unit, step) and not (is_first(i) if kind == "o" else is_last(i)):
                    found.append((n, kind, j, k))
            return found

        def is_first(i):
            return isinstance(i, int) and i == 0

        def is_last(i):
            return isinstance(i, int) and i == B - 1

        def front_uses():
            return [(n, kind, j, k) for n, (_, _, kind, j, k) in enumerate(USES) if kind != "o"]

        def t_of(t, n):
            return not isinstance(t, int) or 0 <= t < n

        def t_in(t):
            return t_of(t, NX)

        def in_pairs(eng, n, step):
            for t in range(2):
                step(t, t)
            with eng.Fori(1, n // 2) as g:
                for p in range(2):
                    step(2 * g + p, p)
            if n % 2:
                step(n - 1, 0)

        def expert_schedule(eng, step):
            for t in range(4):
                step(t, t % 2, t // 2)
            last = NX // 2 - 1
            with eng.Fori(2, last) as g:
                for p in range(2):
                    step(2 * g + p, p, g)
            for t in range(2 * last, NX + 2):
                step(t, t % 2, t // 2)

        @block.sync
        def _(sp):
            def load_xt(i, p):
                sp.dma_start(xt[p][:, :, :], patches[i]).then_inc(xt_in[p], 16)

            def load_txt(i, p):
                sp.dma_start(h0[p][0:NTXT, 2, :], txt[i]).then_inc(txt_in[p], 16)

            sp.dma_start(convT_s[:, :, :], convT).then_inc(w1_in, 16)
            load_xt(0, 0)
            sp.dma_start(posb[:, 0, :], pos[0:R0]).then_inc(w1_in, 16)
            sp.dma_start(posb[0:ROWS[1], 1, :], pos[R0:NPOS]).then_inc(w1_in, 16)
            sp.dma_start(emb_bias[1:R0, 0, :], conv_bias[0:R0 - 1]).then_inc(w1_in, 16)
            sp.dma_start(emb_bias[0:1, 0, :], cls).then_inc(w1_in, 16)
            sp.dma_start(emb_bias[0:ROWS[1], 1, :], conv_bias[0:ROWS[1]]).then_inc(w1_in, 16)
            load_xt(1, 1)
            sp.wait_ge(clear1, 4)
            load_txt(0, 0)
            load_txt(1, 1)

            def store1(i, p, g):
                sp.wait_ge(xn_ok, i + 1)
                sp.dma_start(h0_d[i], h0[p][:, :, :].rearrange("r t d -> r (t d)")).then_inc(h0_out[p], 16)
                sp.wait_ge(hnT_ok, i + 1)
                sp.dma_start(hn_d[i], hnT[p][:, :, :].rearrange("r t d -> r (t d)")).then_inc(hn_out[p], 16)

            with sp.Fori(0, B // 2 - 1) as g:
                for p in range(2):
                    i = 2 * g + p
                    sp.wait_ge(emb_mm, i + 1)
                    load_xt(i + 2, p)
                    store1(i, p, g)
                    sp.wait_ge(h0_out[p], 16 * g + 16)
                    load_txt(i + 2, p)
            for p in range(2):
                store1(B - 2 + p, p, B // 2 - 1)

            for p in range(2):
                sp.wait_ge(hn_out[p], 16 * (B // 2))
                sp.wait_ge(h0_out[p], 16 * (B // 2))
            for dst, src in ((inT_s, inT), (xpT_s, xpT), (dtT_s, dtT), (outT_s, outT), (dww, dw_w), (dwb, dw_b),
                             (dtb, dt_b), (alog, a_logs), (dsk, d_skip)):
                d = dst[tuple(slice(None) for _ in dst.shape)]
                sp.dma_start(d, src).then_inc(w2_in, 16)
            

            sp.wait_ge(zero_ok, 1)
            sp.dma_start(sorted_x.rearrange("(t p) d -> p t d", p=128),
                         zero_s[:, :].unsqueeze(1).to_broadcast([128, NX, D])).then_inc(zero_out, 16)
            if PADDED:
                sp.dma_start(h1_d[T:NT * 128], zero_s[0:NT * 128 - T, :]).then_inc(zero_out, 16)

            def load_hx(i, p):
                sp.dma_start(hx[p][:, :, :].rearrange("r t d -> r (t d)"), hn_d[i]).then_inc(hx_in[p], 16)

            def load_res(i, p):
                sp.dma_start(hres[p][:, :, :].rearrange("r t d -> r (t d)"), h0_d[i]).then_inc(hres_in[p], 16)

            def store_h1(i, p, count):
                sp.wait_ge(misc_free, count)
                for t in range(3):
                    sp.dma_start(h1_d[bass.ds(L * i + OFF[t], ROWS[t])], hres[p][0:ROWS[t], t, :])\
                      .then_inc(h1_out[p], 16)

            def body(i, p, g):
                if not is_last(i):
                    if not is_first(i):
                        sp.wait_ge(misc_full, use_count(i - 1, 8) + 1)
                    load_hx(i + 1, 1 - p)
                if not (isinstance(i, int) and i < 2):
                    sp.wait_ge(h1_out[p], 48 * g)
                load_res(i, p)
                if not is_first(i):
                    store_h1(i - 1, 1 - p, use_count(i, NO))

            load_hx(0, 0)
            body(0, 0, 0)
            body(1, 1, 0)
            body(2, 0, 1)
            if B > 4:
                with sp.Fori(1, B // 2 - 1) as g:
                    body(2 * g + 1, 1, g)
                    body(2 * g + 2, 0, g + 1)
            body(B - 1, 1, B // 2 - 1)
            store_h1(B - 1, 1, LAST_USES + NO)

            for p in range(2):
                sp.wait_ge(h1_out[p], 48 * (B // 2))
            sp.wait_ge(misc_free, LAST_USES + NO)
            sp.wait_ge(zero_out, 32 if PADDED else 16)
            for dst, src in ((rw_s, router_w), (rb_s, router_b)):
                d = dst[tuple(slice(None) for _ in dst.shape)]
                sp.dma_start(d, src).then_inc(wr_in, 16)
            h1_v = h1_d.rearrange("(t p) d -> p t d", p=128)
            for n, (a, b) in enumerate(H1_PARTS):
                sp.dma_start(xn2[:, a:b, :], h1_v[:, a:b, :]).then_inc(h1_in[n], 16)
            for dst, src in ((w1_s, w1), (w2_s, w2), (w3_s, w3)):
                d = dst[tuple(slice(None) for _ in dst.shape)]
                sp.dma_start(d, src).then_inc(w3_in, 16)

            def load_xs(t, p):
                sp.dma_start(xs[p][:, :], sorted_x[bass.ds(128 * t, 128)]).then_inc(xs_in[p], 16)

            sp.wait_ge(scat, 16 * NT)
            load_xs(0, 0)
            load_xs(1, 1)
            sp.dma_start(xn2[:, :, :], h1_v).then_inc(h1_back, 16)

            def next_xs(t, p):
                sp.wait_ge(xsT_ps, t - 1)
                load_xs(t, p)

            with sp.Fori(1, NX // 2) as g:
                for p in range(2):
                    next_xs(2 * g + p, p)
            if NX % 2:
                next_xs(NX - 1, 0)
            for p in range(2):
                sp.wait_ge(ys_out[p], 16 * ((NX + 1 - p) // 2))
            for a in range(0, NT, GROUP):
                b = min(a + GROUP, T // 128)
                sp.wait_ge(fin_ok, min(a + GROUP, NT))
                if b > a:
                    sp.dma_start(out[128 * a:128 * b].rearrange("(t p) d -> p t d", p=128), xn2[:, a:b, :])\
                      .then_inc(fin_out, 16)
            if T % 128:
                sp.dma_start(out[T - T % 128:T], xn2[0:T % 128, NT - 1, :]).then_inc(fin_out, 16)
            sp.wait_ge(fin_out, 16 * (len([a for a in range(0, NT, GROUP) if T // 128 > a]) + (T % 128 > 0)))

        @block.gpsimd
        def _(gp):
            gp.memset(zero_s[:, :], 0.0).then_inc(zero_ok, 1)
            gp.memset(ident[:, :], 0.0).then_inc(gp_set, 1)
            gp.wait_ge(gp_set, 1)
            gp.affine_select(out=ident[:, :], in_=ident[:, :], compare_op=ALU.not_equal, fill=1.0, base=0,
                             pattern=[[-1, 128]], channel_multiplier=1).then_inc(gp_set, 1)
            gp.wait_ge(hnT_ok, B)
            gp.wait_ge(xn_ok, B)
            for p in range(2):
                gp.wait_ge(hn_out[p], 16 * (B // 2))
                gp.wait_ge(h0_out[p], 16 * (B // 2))
            gp.memset(sel[:, :, :], 0.0).then_inc(gp_set, 1)
            for part in range(3):
                gp.wait_ge(gp_set, 3 + part)
                gp.affine_select(out=sel[:, :, :], in_=sel[:, :, :], compare_op=ALU.not_equal, fill=1.0,
                                 base=-32 * part, pattern=[[-1, 2 * NS], [0, 128]], channel_multiplier=1)\
                  .then_inc(gp_set, 1)
            for buf in (dA[0], dA[1], h_s):
                gp.memset(buf[:, :, :, 0:1], 0.0).then_inc(pads, 1)

            def split_bc(i, k, p):
                base = 4 * (2 * i + k)
                gp.wait_ge(misc_free, use_count(None if is_first(i) else i - 1, 10 + k) + 1)
                hi, lo = bcs[p][32:64, k, :], bcs[p][64:96, k, :]
                gp.tensor_tensor(rest1[64:96, :], bcf[64:96, k, :], lo, ALU.subtract).then_inc(split, 1)
                gp.tensor_tensor(mid[64:96, :], bcf[64:96, k, :], lo, ALU.subtract).then_inc(split, 1)
                gp.tensor_tensor(hi, bcf[32:64, k, :], hi, ALU.subtract).then_inc(split, 1)
                gp.wait_ge(split, base + 2)
                gp.tensor_tensor(lo, rest1[64:96, :], mid[64:96, :], ALU.subtract).then_inc(split, 1)
                gp.wait_ge(split, base + 4)

            def delta_du(i, k, p):
                gp.wait_ge(sp_ln, 2 * i + k + 1)
                if not is_first(i):
                    gp.wait_ge(da_ok, 3 * (4 * (i - 1) + 2 * k + 2))
                gp.tensor_tensor(delta[:, k, :, :], relx[:, :, :], absx[:, :, :], ALU.add).then_inc(delta_ok, 1)
                gp.wait_ge(delta_ok, 2 * i + k + 1)
                gp.wait_ge(u_ok, i + 1)
                if not (isinstance(i, int) and i < 2):
                    gp.wait_ge(dbu, 3 * PAIRS * 4 * (i - 1))
                gp.tensor_tensor(du[p][:, k, :, :], delta[:, k, :, :], u_s[:, :, :], ALU.mult).then_inc(du_ok, 1)

            def body(i, p):
                for k in range(2):
                    split_bc(i, k, p)
                for k in range(2):
                    delta_du(i, k, p)

            body(0, 0)
            body(1, 1)
            if B > 2:
                with gp.Fori(1, B // 2) as g:
                    body(2 * g, 0)
                    body(2 * g + 1, 1)

            gp.wait_ge(h1_in[0], 16)
            gp.memset(ones[:, :], 1.0).then_inc(gp_set, 1)
            gp.wait_ge(gp_set, 7)
            gp.affine_select(out=tri[:, :], in_=ones[:, :], compare_op=ALU.is_gt, fill=0.0, base=0,
                             pattern=[[1, 128]], channel_multiplier=-1).then_inc(gp_set, 1)
            gp.iota(start_f[:, :], pattern=[[128, NX]], base=0, channel_multiplier=0,
                    allow_small_or_imprecise_dtypes=True).then_inc(gp_set, 1)
            gp.iota(prio[:, :], pattern=[[-1, E]], base=E, channel_multiplier=0,
                    allow_small_or_imprecise_dtypes=True).then_inc(gp_set, 1)
            gp.wait_ge(route, ROUTE_ALL)
            for t in range(NT):
                gp.indirect_dma_start(sorted_x, bass.IndirectOffsetOnAxis(ap=slot_u[:, t:t + 1], axis=0),
                                      xn2[:, t, :], None).then_inc(scat, 16)

            def store_ys(t, p):
                gp.wait_ge(ys_ok, t + 1)
                gp.dma_start(sorted_y[bass.ds(128 * t, 128)], ys[p][:, :]).then_inc(ys_out[p], 16)

            in_pairs(gp, NX, store_ys)
            for p in range(2):
                gp.wait_ge(ys_out[p], 16 * ((NX + 1 - p) // 2))
            for t in range(NT):
                gp.indirect_dma_start(yr[:, t, :], None, sorted_y,
                                      bass.IndirectOffsetOnAxis(ap=slot_u[:, t:t + 1], axis=0)).then_inc(yr_in, 16)

        @block.scalar
        def _(act):
            def ln1(i, p, g):
                act.wait_ge(st_chain, 11 * i + 10)
                act.activation(rt[p][:, :], sd[p][:, 4, :], ACT.Sqrt).then_inc(sqrt_ok, 1)
                act.wait_ge(tr_ok, i + 1)
                if not (isinstance(i, int) and i < 2):
                    act.wait_ge(hn_out[p], 16 * g)
                act.activation(hnT[p][:, :, :], tr_ps[0:DH, p, :, 0:L], ACT.Copy).then_inc(hnT_ok, 1)

            ln1(0, 0, 0)
            ln1(1, 1, 0)
            with act.Fori(1, B // 2) as g:
                for p in range(2):
                    ln1(2 * g + p, p, g)

            act.wait_ge(w2_in, 16 * W2_DMAS)
            act.activation(a_neg[:, :, :], alog[:, :, :], ACT.Exp).then_inc(set2, 1)
            act.wait_ge(set2, 3)

            def take(i, n, kind, j, k, p):
                count = use_count(i, n)
                nxt = 0 if i is None else i + 1
                act.wait_ge(misc_full, count + 1)
                if kind == "x":
                    if i is not None:
                        act.wait_ge(u_ok, nxt)
                    act.activation(xc[:, j, :], misc[:, 0:L], ACT.Identity, bias=dwb[:, j:j + 1],
                                   scale=dww[:, j, 1:2]).then_inc(xc_mid, 1)
                elif kind == "z":
                    if j == 0 and i is not None and not is_first(i):
                        act.wait_ge(gated, 3 * i)
                    act.activation(z_s[p][:, j, :], misc[:, 0:L], ACT.Copy).then_inc(misc_free, 1)
                elif kind == "dt":
                    act.activation(dt_in[:, :], misc[0:dtT.shape[0], 0:L], ACT.Copy).then_inc(misc_free, 1)
                elif kind == "bc":
                    if i is not None:
                        act.wait_ge(split, 4 * (2 * (nxt - 1) + k + 1))
                    act.activation(bcf[:, k, :], misc[0:96, 0:L], ACT.Copy).then_inc(bcf_ok, 1)
                    if i is not None and not is_first(i):
                        act.wait_ge(bc_full, 8 * 4 * (nxt - 1))
                    act.wait_ge(bcf_ok, 2 * nxt + k + 1)
                    act.activation(bcs[p][:, k, :], misc[0:96, 0:L], ACT.Copy).then_inc(misc_free, 1)
                elif kind == "p":
                    if j == 0 and not (i is None and k == 0):
                        act.wait_ge(delta_ok, 2 * nxt + k)
                    b = dtb[:, J * k + j:J * k + j + 1]
                    act.activation(absx[:, j, :], misc[:, 0:L], ACT.Abs, bias=b).then_inc(sp_exp, 1)
                    act.activation(relx[:, j, :], misc[:, 0:L], ACT.Relu, bias=b).then_inc(misc_free, 1)
                    if j == 2:
                        c = 4 * (2 * nxt + k)
                        act.wait_ge(sp_exp, c + 3)
                        act.activation(absx[:, :, :], absx[:, :, :], ACT.Exp, scale=-1.0).then_inc(sp_exp, 1)
                        act.wait_ge(sp_exp, c + 4)
                        act.wait_ge(misc_free, count + 1)
                        act.activation(absx[:, :, :], absx[:, :, :], ACT.Ln, bias=1.0).then_inc(sp_ln, 1)

            def silu(nxt, i):
                act.wait_ge(misc_free, use_count(i, 8) + 1)
                if i is not None:
                    act.wait_ge(skip_ok, nxt)
                    act.wait_ge(du_ok, 2 * nxt)
                act.activation(u_s[:, :, :], xc[:, :, :], ACT.Silu).then_inc(u_ok, 1)
                act.preload_act_table_set("natural_log_exp_and_others")

            def exps(i, unit, items):
                k, half = unit // 2, unit % 2
                v = unit % 2
                V = 4 * i + unit
                for m in items:
                    j, n = m // HN, m % HN
                    if n == 0:
                        act.wait_ge(delta_ok, 2 * i + k + 1)
                        if not (isinstance(V, int) and V < 2):
                            act.wait_ge(scan_ok, 3 * (V - 2) + j + 1)
                    a = a_neg[:, J * k + j, half * HN + n:half * HN + n + 1]
                    e = act.activation(dA[v][:, j, n, 1:L + 1], delta[:, k, j, :], ACT.Exp, scale=a)
                    if n == HN - 1:
                        e.then_inc(da_ok, 1)

            def body(i, p):
                for unit in range(4):
                    for step in range(8):
                        if (unit, step) == (2, 0) and not is_last(i):
                            silu(i + 1, i)
                        items = range(3 * step, 3 * step + 3)
                        if unit < 3:
                            exps(i, unit + 1, items)
                        elif not is_last(i):
                            exps(i + 1, 0, items)
                        for n, kind, j, k in uses_at(i, unit, step):
                            if kind != "o":
                                take(i, n, kind, j, k, 1 - p)

            for n, kind, j, k in front_uses():
                if kind == "dt":
                    silu(0, None)
                take(None, n, kind, j, k, 0)
            act.wait_ge(pads, 3)
            exps(0, 0, range(J * HN))
            body(0, 0)
            if B > 2:
                with act.Fori(0, B // 2 - 1) as g:
                    body(2 * g + 1, 1)
                    body(2 * g + 2, 0)
            body(B - 1, 1)

            act.wait_ge(ln2, LN2_VAR)
            act.activation(root[:, :], stat[:, 4, :], ACT.Sqrt).then_inc(sqrt2, 1)

            def x2T_copy(t, p):
                act.wait_ge(tr2_ok, t + 1)
                if not (isinstance(t, int) and t < 2):
                    act.wait_ge(lg_ok, t - 1)
                act.activation(x2T[p][:, :, :], tr3[0:DH, p, 0:256].rearrange("p (a b) -> p a b", a=2),
                               ACT.Copy).then_inc(x2T_ok, 1)

            in_pairs(act, NT, x2T_copy)
            act.wait_ge(route, ROUTE_LT)
            act.activation(lt[:, :, :], lt[:, :, :], ACT.Exp).then_inc(rexp, 1)

            def xsT_copy(t, p):
                act.wait_ge(xsT_ps, t + 1)
                if not (isinstance(t, int) and t < 2):
                    act.wait_ge(up_ok, t - 1)
                act.activation(xsT[p][:, :, :], tr3[0:DH, p, 0:256].rearrange("p (a b) -> p a b", a=2),
                               ACT.Copy).then_inc(xsT_ok, 1)

            def expert(t, p, g):
                if t_in(t):
                    act.wait_ge(up_ok, t + 1)
                    if not (isinstance(t, int) and t < 2):
                        act.wait_ge(act_ok, t - 1)
                    act.activation(g1[p][:, :], up_ps[:, p, 0, :], ACT.Silu).then_inc(g1_ok, 1)
                if t_in(t + 2):
                    xsT_copy(t + 2, p)
                if t_in(t - 1):
                    act.wait_ge(actT_ps, t)
                    if not (isinstance(t, int) and t < 3):
                        act.wait_ge(dn_ok, t - 2)
                    act.activation(actT[1 - p][:, :, :], at_ps[:, :].rearrange("p (a b) -> p a b", a=HC), ACT.Copy)\
                       .then_inc(actT_ok, 1)

            xsT_copy(0, 0)
            xsT_copy(1, 1)
            expert_schedule(act, expert)

        @block.tensor
        def _(pe):
            def embed(i, p, g):
                pe.wait_ge(xt_in[p], 16 * g + 16)
                if not (isinstance(i, int) and i < 2):
                    pe.wait_ge(h0_ok, i - 1)
                for t in range(2):
                    for c in range(KC):
                        mm = pe.matmul(emb_ps[0:ROWS[t], p, t, 0:D], xt[p][:, c, OFF[t]:OFF[t] + ROWS[t]],
                                       convT_s[:, c, :], start=(c == 0), stop=(c == KC - 1))
                mm.then_inc(emb_mm, 1)

            def transpose1(i, p):
                pe.wait_ge(xn_ok, i + 1)
                if not (isinstance(i, int) and i < 2):
                    pe.wait_ge(hnT_ok, i - 1)
                for t in range(3):
                    for h in range(2):
                        mm = pe.transpose(tr_ps[0:DH, p, h, OFF[t]:OFF[t] + ROWS[t]],
                                          xn[p][0:ROWS[t], t, DH * h:DH * h + DH], ident[0:ROWS[t], 0:ROWS[t]])
                mm.then_inc(tr_ok, 1)

            pe.wait_ge(w1_in, 16 * W1_DMAS)
            pe.wait_ge(gp_set, 2)
            embed(0, 0, 0)
            embed(1, 1, 0)
            transpose1(0, 0)

            def embed_pair(i, g):
                embed(i + 2, 0, g + 1)
                transpose1(i + 1, 1)
                embed(i + 3, 1, g + 1)
                transpose1(i + 2, 0)

            embed_pair(0, 0)
            with pe.Fori(1, B // 2 - 1) as g:
                embed_pair(2 * g, g)
            transpose1(B - 1, 1)

            def put(i, n, kind, j, k, p, g):
                count = use_count(i, n)
                nxt = 0 if i is None else i + 1
                if not (isinstance(count, int) and count == 0):
                    pe.wait_ge(misc_free, count)
                if kind == "x" or kind == "z":
                    if kind == "z" and j == 0:
                        pe.wait_ge(hx_in[p], 16 * g + 16)
                    c0 = 128 * j + (J * 128 if kind == "z" else 0)
                    for h in range(2):
                        mm = pe.matmul(misc[:, 0:L], inT_s[:, h, c0:c0 + 128], hx[p][:, h, :],
                                       start=(h == 0), stop=(h == 1))
                elif kind == "dt" or kind == "bc":
                    if kind == "dt":
                        pe.wait_ge(u_ok, nxt + 1)
                        c0, m = 192, dtT.shape[0]
                    else:
                        c0, m = 96 * k, 96
                    for jj in range(J):
                        mm = pe.matmul(misc[0:m, 0:L], xpT_s[:, jj, c0:c0 + m], u_s[:, jj, :],
                                       start=(jj == 0), stop=(jj == J - 1))
                elif kind == "p":
                    r = slice(64 * k, 64 * k + RANK)
                    mm = pe.matmul(misc[:, 0:L], dtT_s[r, 128 * j:128 * j + 128], dt_in[r, :], start=True, stop=True)
                elif kind == "o":
                    pe.wait_ge(gated, 3 * i)
                    for jj in range(J):
                        mm = pe.matmul(misc[0:ROWS[j], 0:D], yg[:, jj, OFF[j]:OFF[j] + ROWS[j]], outT_s[:, jj, :],
                                       start=(jj == 0), stop=(jj == J - 1))
                mm.then_inc(misc_full, 1)

            def broadcast(i, unit, step, p):
                U = 4 * i + unit
                k, half = unit // 2, unit % 2
                if unit % 2 == 0 and step == 0:
                    pe.wait_ge(split, 4 * (2 * i + k + 1))
                if step >= 6:
                    pe.wait_ge(hc_full, 12 * U + 3 * (step - 6) + 3)
                elif step >= 2:
                    pe.wait_ge(dbu, 12 * U + 3 * (step - 2) + 3)
                elif not (isinstance(U, int) and U == 0):
                    pe.wait_ge(hc_full, 12 * (U - 1) + 3 * (step + 2) + 3)
                for m in range(2):
                    n = (0 if step < 4 else NS) + half * HN + 2 * (step % 4) + m
                    mm = pe.matmul(bc_ps[:, step % 2, m, 0:L], sel[:, n, :], bcs[p][:, k, :], start=True, stop=True)
                mm.then_inc(bc_full, 1)

            def accumulate(i, unit, n):
                for m in range(2):
                    if m == 0:
                        pe.wait_ge(hc_full, 12 * (4 * i + unit) + n + 1)
                    mm = pe.matmul(y_ps[:, n % 3, 0:L], ident[:, :], hc[:, n % RING, m, :],
                                   start=False, stop=unit == 3 and n >= 3 * (PAIRS - 1) and m == 1)
                mm.then_inc(hc_free, 1)

            def sums_at(i, unit, step):
                first = 0
                for at, count in SUMS:
                    for n in range(first, first + count):
                        if at == step:
                            accumulate(i, unit, n)
                        elif at == step + 8 and unit > 0:
                            accumulate(i, unit - 1, n)
                        elif at == step + 8 and not is_first(i):
                            accumulate(i - 1, 3, n)
                    first += count

            def skip(i):
                if not is_first(i):
                    pe.wait_ge(gated, 3 * i)
                for j in range(J):
                    mm = pe.matmul(y_ps[:, j, 0:L], diag_d[:, j, :], u_s[:, j, :], start=True, stop=False)
                mm.then_inc(skip_ok, 1)

            def body(i, p, g):
                for unit in range(4):
                    for step in range(8):
                        broadcast(i, unit, step, p)
                        if unit == 0 and step == 4:
                            skip(i)
                        sums_at(i, unit, step)
                        for n, kind, j, k in uses_at(i, unit, step):
                            put(i, n, kind, j, k, 1 - p, g + p)

            pe.wait_ge(w2_in, 16 * W2_DMAS)
            pe.wait_ge(set2, 3 + J)
            pe.wait_ge(gp_set, 6)
            pe.wait_ge(hnT_ok, B)
            for n, kind, j, k in front_uses():
                put(None, n, kind, j, k, 0, 0)
            body(0, 0, 0)
            if B > 2:
                with pe.Fori(0, B // 2 - 1) as g:
                    body(2 * g + 1, 1, g)
                    body(2 * g + 2, 0, g + 1)
            body(B - 1, 1, B // 2 - 1)
            for step in range(3):
                sums_at(B, 0, step)
            for t in range(NO):
                put(B, t, "o", t, 0, 0, 0)

            pe.wait_ge(wr_in, 32)

            def tile2(t, p):
                if t_of(t, NT):
                    pe.wait_ge(xn2_ok, t + 1)
                    if not (isinstance(t, int) and t < 2):
                        pe.wait_ge(x2T_ok, t - 1)
                    for h in range(2):
                        mm = pe.transpose(tr3[0:DH, p, 128 * h:128 * h + 128],
                                          xn2[:, bass.ds(t, 1), DH * h:DH * h + DH].rearrange("p o d -> p (o d)"),
                                          ident[:, :])
                    mm.then_inc(tr2_ok, 1)
                if t_of(t - 1, NT):
                    pe.wait_ge(x2T_ok, t)
                    b, c = (t - 1) // TB, (t - 1) % TB
                    for h in range(2):
                        mm = pe.matmul(lg_ps[:, b, E * c:E * c + E], x2T[1 - p][:, h, :], rw_s[:, h, :],
                                       start=(h == 0), stop=(h == 1), skip_group_check=True)
                    mm.then_inc(lg_ok, 1)

            for t in range(NT + 1):
                tile2(t, t % 2)
            pe.wait_ge(route, ROUTE_HOT)
            pe.wait_ge(gp_set, 10)
            oh = onehot[:, :, :].rearrange("p t e -> p (t e)")
            for ops, out_ps in ((tri, [lg_ps[:, n, :] for n in range(2)]), (ones, [b[:, :] for b in cnt_ps])):
                for n in range(NB):
                    a, b = 512 * n, min(512 * n + 512, NT * E)
                    mm = pe.matmul(out_ps[n][:, 0:b - a], ops[:, :], oh[:, a:b], start=True, stop=True)
            mm.then_inc(rank_ok, 1)
            pe.wait_ge(route, ROUTE_ALL)

            def expert_of(t):
                return pe.value_load(texp_i[0:1, bass.ds(t, 1)], min_val=0, max_val=E - 1)

            def transpose_x(t, p, g):
                pe.wait_ge(xs_in[p], 16 * g + 16)
                if not (isinstance(t, int) and t < 2):
                    pe.wait_ge(xsT_ok, t - 1)
                for h in range(2):
                    mm = pe.transpose(tr3[0:DH, p, 128 * h:128 * h + 128], xs[p][:, DH * h:DH * h + DH], ident[:, :])
                mm.then_inc(xsT_ps, 1)

            def expert(t, p, g):
                if t_in(t):
                    e = expert_of(t)
                    pe.wait_ge(xsT_ok, t + 1)
                    if not (isinstance(t, int) and t < 2):
                        pe.wait_ge(act_ok, t - 1)
                    for n, w in enumerate((w1_s, w2_s)):
                        for h in range(2):
                            mm = pe.matmul(up_ps[:, p, n, :], xsT[p][:, h, :],
                                           w[:, h, bass.ds(e, 1), :].rearrange("p o h -> p (o h)"),
                                           start=(h == 0), stop=(h == 1))
                    mm.then_inc(up_ok, 1)
                if t_in(t + 2):
                    transpose_x(t + 2, p, g + 1)
                if t_in(t - 1):
                    pe.wait_ge(act_ok, t)
                    if not (isinstance(t, int) and t < 2):
                        pe.wait_ge(actT_ok, t - 1)
                    for c in range(HC):
                        mm = pe.transpose(at_ps[:, 128 * c:128 * c + 128], act_s[1 - p][:, 128 * c:128 * c + 128],
                                          ident[:, :])
                    mm.then_inc(actT_ps, 1)
                if t_in(t - 2):
                    e = expert_of(t - 2)
                    pe.wait_ge(actT_ok, t - 1)
                    if not (isinstance(t, int) and t < 3):
                        pe.wait_ge(ys_ok, t - 2)
                    for c in range(HC):
                        mm = pe.matmul(dn_ps[:, 0:D], actT[p][:, c, :],
                                       w3_s[:, c, bass.ds(e, 1), :].rearrange("p o h -> p (o h)"),
                                       start=(c == 0), stop=(c == HC - 1))
                    mm.then_inc(dn_ok, 1)

            pe.wait_ge(w3_in, 16 * W3_DMAS)
            transpose_x(0, 0, 0)
            transpose_x(1, 1, 0)
            expert_schedule(pe, expert)

        @block.vector
        def _(dve):
            for n, b in enumerate((h0[0], h0[1], xn[0], xn[1])):
                dve.memset(b[:, :, :], 0.0).then_inc(clear1, 1)
            dve.wait_ge(w1_in, 16 * W1_DMAS)
            for t in range(2):
                dve.tensor_tensor(posb[0:ROWS[t], t, :], posb[0:ROWS[t], t, :], emb_bias[0:ROWS[t], t, :], ALU.add)\
                   .then_inc(posb_ok, 1)
            dve.wait_ge(posb_ok, 2)
            dve.wait_ge(clear1, 4)

            def embed(i, p, g):
                dve.wait_ge(emb_mm, i + 1)
                if not (isinstance(i, int) and i < 2):
                    dve.wait_ge(h0_out[p], 16 * g)
                for t in range(2):
                    a = dve.tensor_tensor(h0[p][0:ROWS[t], t, :], emb_ps[0:ROWS[t], p, t, 0:D],
                                          posb[0:ROWS[t], t, :], ALU.add)
                a.then_inc(h0_ok, 1)
                dve.wait_ge(h0_ok, i + 1)
                dve.wait_ge(txt_in[p], 16 * g + 16)
                for t in range(3):
                    dve.bn_stats(bst[p][:, t, :], h0[p][:, t, :]).then_inc(st_chain, 1)
                me, se, mo, so = (bst[p][:, :, c] for c in (1, 2, 4, 5))
                total, diff, sq, mean, var, inv = (sd[p][:, c, :] for c in range(6))
                dve.wait_ge(st_chain, 11 * i + 3)
                dve.tensor_tensor(total, me, mo, ALU.add).then_inc(st_chain, 1)
                dve.tensor_tensor(diff, me, mo, ALU.subtract).then_inc(st_chain, 1)
                dve.tensor_tensor(sq, se, so, ALU.add).then_inc(st_chain, 1)
                dve.wait_ge(st_chain, 11 * i + 6)
                dve.tensor_scalar(mean, total, 0.5, None, ALU.mult).then_inc(st_chain, 1)
                dve.tensor_tensor(diff, diff, diff, ALU.mult).then_inc(st_chain, 1)
                dve.tensor_scalar(var, sq, 1.0 / D, EPS, ALU.mult, ALU.add).then_inc(st_chain, 1)
                dve.wait_ge(st_chain, 11 * i + 9)
                dve.scalar_tensor_tensor(var, diff, 0.25, var, ALU.mult, ALU.add).then_inc(st_chain, 1)
                dve.wait_ge(sqrt_ok, i + 1)
                dve.reciprocal(inv, rt[p][:, :]).then_inc(st_chain, 1)
                dve.wait_ge(st_chain, 11 * i + 11)
                if not (isinstance(i, int) and i < 2):
                    dve.wait_ge(tr_ok, i - 1)
                for t in range(3):
                    a = dve.tensor_scalar(xn[p][:, t, :], h0[p][:, t, :], sd[p][:, 3, t:t + 1], sd[p][:, 5, t:t + 1],
                                          ALU.subtract, ALU.mult)
                a.then_inc(xn_ok, 1)

            embed(0, 0, 0)
            embed(1, 1, 0)
            if B > 2:
                with dve.Fori(1, B // 2) as g:
                    for p in range(2):
                        embed(2 * g + p, p, g)

            dve.wait_ge(w2_in, 16 * W2_DMAS)
            dve.wait_ge(set2, 1)
            dve.tensor_scalar(a_neg[:, :, :], a_neg[:, :, :], -1.0, None, ALU.mult).then_inc(set2, 1)
            dve.tensor_tensor(dsum[:, :], dsk[:, 0:J], dsk[:, J:2 * J], ALU.add).then_inc(set2, 1)
            dve.wait_ge(set2, 3)
            dve.wait_ge(gp_set, 2)
            for j in range(J):
                dve.tensor_scalar(diag_d[:, j, :], ident[:, :], dsum[:, j:j + 1], None, ALU.mult).then_inc(set2, 1)
            dve.wait_ge(pads, 3)

            def conv(i, n, j):
                nxt = 0 if i is None else i + 1
                dve.wait_ge(xc_mid, 3 * nxt + j + 1)
                dve.scalar_tensor_tensor(xc[:, j, 1:L], misc[:, 0:L - 1], dww[:, j, 0:1], xc[:, j, 1:L],
                                         ALU.mult, ALU.add).then_inc(xc_left, 1)
                dve.wait_ge(xc_left, 3 * nxt + j + 1)
                dve.scalar_tensor_tensor(xc[:, j, 0:L - 1], misc[:, 1:L], dww[:, j, 2:3], xc[:, j, 0:L - 1],
                                         ALU.mult, ALU.add).then_inc(misc_free, 1)

            def gate(i, p):
                dve.wait_ge(hc_free, 3 * PAIRS * 4 * (i + 1))
                dve.wait_ge(misc_full, use_count(i, NO))
                for j in range(J):
                    dve.tensor_tensor(yg[:, j, :], y_ps[:, j, 0:L], z_s[p][:, j, :], ALU.mult).then_inc(gated, 1)

            def residual(i, p, g, t, count):
                dve.wait_ge(misc_full, count + 1)
                if t == 0:
                    dve.wait_ge(hres_in[p], 16 * g + 16)
                dve.tensor_tensor(hres[p][0:ROWS[t], t, :], misc[0:ROWS[t], 0:D], hres[p][0:ROWS[t], t, :], ALU.add)\
                   .then_inc(misc_free, 1)

            between = [[(n, kind, jj, kk) for n, (a, _, kind, jj, kk) in enumerate(USES) if (a, jj) == divmod(m, J)]
                       for m in range(4 * J)]

            def body(i, p, g):
                for unit in range(4):
                    k, U = unit // 2, 4 * i + unit
                    hp = h_s[:, :, :, 1:L + 1]
                    for step in range(8):
                        if step != 4:
                            dve.wait_ge(bc_full, 8 * U + step + 1)
                        slot = bc_ps[:, step % 2, :, 0:L]
                        q = step % 4
                        if step == 0:
                            if unit % 2 == 0:
                                dve.wait_ge(du_ok, 2 * i + k + 1)
                            dve.wait_ge(hc_full, 12 * U)
                        if step == 4:
                            for j in range(J):
                                dve.wait_ge(dbu, 12 * U + 9 + j + 1)
                                dve.wait_ge(da_ok, 3 * U + j + 1)
                                a = dA[unit % 2][:, j, :, :].rearrange("p n t -> p (n t)")
                                b = h_s[:, j, :, :].rearrange("p n t -> p (n t)")
                                if k == 1:
                                    a, b = a[:, ::-1], b[:, ::-1]
                                dve.tensor_tensor_scan(b, a, b, 0.0, ALU.mult, ALU.add).then_inc(scan_ok, 1)
                                for n, kind, jj, kk in between[unit * J + j]:
                                    if kind == "x" and not is_last(i):
                                        conv(i, n, jj)
                                    elif kind == "o" and not is_first(i):
                                        residual(i - 1, 1 - p, g + p - 1, jj, use_count(i, n))
                            dve.wait_ge(bc_full, 8 * U + step + 1)
                        for j in range(J):
                            hq = hp[:, j, 2 * q:2 * q + 2, :]
                            if step < 4:
                                d2 = du[p][:, k, j:j + 1, :].to_broadcast([128, 2, L])
                                dve.tensor_tensor(hq, slot, d2, ALU.mult).then_inc(dbu, 1)
                            else:
                                if q == 0:
                                    dve.wait_ge(scan_ok, 3 * U + j + 1)
                                n = 12 * U + 3 * q + j + 1 - RING
                                if not (isinstance(n, int) and n <= 0):
                                    dve.wait_ge(hc_free, n)
                                dve.tensor_tensor(hc[:, (3 * q + j) % RING, :, :], hq, slot, ALU.mult)\
                                   .then_inc(hc_full, 1)
                        if unit == 0 and step == 3 and not is_first(i):
                            gate(i - 1, 1 - p)

            for n, kind, j, k in front_uses():
                if kind == "x":
                    conv(None, n, j)
            body(0, 0, 0)
            if B > 2:
                with dve.Fori(0, B // 2 - 1) as g:
                    body(2 * g + 1, 1, g)
                    body(2 * g + 2, 0, g + 1)
            body(B - 1, 1, B // 2 - 1)
            gate(B - 1, 1)
            for t in range(3):
                residual(B - 1, 1, B // 2 - 1, t, LAST_USES + t)

            for n, (a, b) in enumerate(H1_PARTS):
                dve.wait_ge(h1_in[n], 16)
                with dve.Fori(a, b) as t:
                    dve.bn_stats(bst2[:, bass.ds(t, 1), :].rearrange("p o s -> p (o s)"),
                                 xn2[:, bass.ds(t, 1), :].rearrange("p o d -> p (o d)")).then_inc(ln2, 1)
            ln2_count = [NT]

            def ln_step(ins):
                ins.then_inc(ln2, 1)
                ln2_count[0] += 1
                dve.wait_ge(ln2, ln2_count[0])

            dve.wait_ge(ln2, NT)
            me, se, mo, so = (bst2[:, :, c] for c in (1, 2, 4, 5))
            ln_step(dve.tensor_tensor(stat[:, 0, :], me, mo, ALU.add))
            ln_step(dve.tensor_tensor(stat[:, 1, :], me, mo, ALU.subtract))
            ln_step(dve.tensor_tensor(stat[:, 2, :], se, so, ALU.add))
            ln_step(dve.tensor_scalar(stat[:, 3, :], stat[:, 0, :], 0.5, None, ALU.mult))
            ln_step(dve.tensor_tensor(stat[:, 1, :], stat[:, 1, :], stat[:, 1, :], ALU.mult))
            ln_step(dve.tensor_scalar(stat[:, 4, :], stat[:, 2, :], 1.0 / D, EPS, ALU.mult, ALU.add))
            ln_step(dve.scalar_tensor_tensor(stat[:, 4, :], stat[:, 1, :], 0.25, stat[:, 4, :], ALU.mult, ALU.add))
            assert ln2_count[0] == LN2_VAR
            dve.wait_ge(sqrt2, 1)
            ln_step(dve.reciprocal(stat[:, 5, :], root[:, :]))
            with dve.Fori(0, NT) as t:
                x = xn2[:, bass.ds(t, 1), :].rearrange("p o d -> p (o d)")
                dve.tensor_scalar(x, x, stat[:, 3, bass.ds(t, 1)], stat[:, 5, bass.ds(t, 1)], ALU.subtract, ALU.mult)\
                   .then_inc(xn2_ok, 1)

            done = [0]

            def step(ins):
                ins.then_inc(route, 1)
                done[0] += 1
                dve.wait_ge(route, done[0])

            def over_e(x, n=NT):
                return x.unsqueeze(2).to_broadcast([128, n, E])

            dve.wait_ge(lg_ok, NT)
            dve.wait_ge(wr_in, 32)
            for n in range(NB):
                a, b = TB * n, min(TB * n + TB, NT)
                step(dve.tensor_tensor(lg[:, a:b, :], lg_ps[:, n, 0:E * (b - a)].rearrange("p (t e) -> p t e", e=E),
                                       rb_s[:, :].unsqueeze(1).to_broadcast([128, b - a, E]), ALU.add))
            step(dve.tensor_reduce(lmax[:, :], lg[:, :, :], AX.X, ALU.max))
            step(dve.tensor_tensor(lt[:, :, :], lg[:, :, :], over_e(lmax[:, :]), ALU.subtract))
            dve.wait_ge(gp_set, 10)
            step(dve.scalar_tensor_tensor(onehot[:, :, :], lt[:, :, :], 0.0,
                                          prio[:, :].unsqueeze(1).to_broadcast([128, NT, E]), ALU.is_equal, ALU.mult))
            assert done[0] == ROUTE_LT
            step(dve.tensor_reduce(best[:, :], onehot[:, :, :], AX.X, ALU.max))
            step(dve.tensor_tensor(onehot[:, :, :], onehot[:, :, :], over_e(best[:, :]), ALU.is_equal))
            assert done[0] == ROUTE_HOT
            dve.wait_ge(rexp, 1)
            step(dve.tensor_reduce(lmax[:, :], lt[:, :, :], AX.X, ALU.add))
            step(dve.reciprocal(prob[:, :], lmax[:, :]))
            dve.wait_ge(rank_ok, 1)
            for n in range(NB):
                a, b = TB * n, min(TB * n + TB, NT)
                step(dve.tensor_copy(rank_e[:, a:b, :], lg_ps[:, n, 0:E * (b - a)].rearrange("p (t e) -> p t e", e=E)))
                step(dve.tensor_copy(cnt[:, :, a:b],
                                     cnt_ps[n][:, 0:E * (b - a)].rearrange("p (t e) -> p e t", e=E)))
            step(dve.memset(cum[:, :, 0:1], 0.0))
            for e in range(E):
                step(dve.tensor_tensor_scan(cum[:, e, 1:NT + 1], ones[:, 0:NT], cnt[:, e, :], 0.0, ALU.mult, ALU.add))
            step(dve.tensor_scalar(tot_i[:, :], cum[:, :, NT], 127.0, None, ALU.add))
            step(dve.tensor_scalar(tot_i[:, :], tot_i[:, :], -128, None, ALU.bitwise_and))
            step(dve.tensor_copy(pad_f[:, :], tot_i[:, :]))
            step(dve.memset(ends[:, 0:1], 0.0))
            step(dve.tensor_tensor_scan(ends[:, 1:E + 1], ones[:, 0:E], pad_f[:, :], 0.0, ALU.mult, ALU.add))
            step(dve.tensor_tensor(rank_e[:, :, :], rank_e[:, :, :], cum[:, :, 0:NT].rearrange("p e t -> p t e"), ALU.add))
            step(dve.tensor_tensor(rank_e[:, :, :], rank_e[:, :, :],
                                   ends[:, 0:E].unsqueeze(1).to_broadcast([128, NT, E]), ALU.add))
            step(dve.tensor_tensor(rank_e[:, :, :], rank_e[:, :, :], onehot[:, :, :], ALU.mult))
            step(dve.tensor_reduce(slot_f[:, :], rank_e[:, :, :], AX.X, ALU.add))
            step(dve.tensor_copy(slot_u[:, :], slot_f[:, :]))
            step(dve.memset(texp[:, :], 0.0))
            for e in range(1, E):
                step(dve.scalar_tensor_tensor(texp[:, :], start_f[:, :], ends[0:1, e:e + 1], texp[:, :],
                                              ALU.is_ge, ALU.add))
            step(dve.tensor_copy(texp_i[:, :], texp[:, :]))
            assert done[0] == ROUTE_ALL, (done[0], ROUTE_ALL)

            def expert(t, p, g):
                if t_in(t):
                    dve.wait_ge(g1_ok, t + 1)
                    if not (isinstance(t, int) and t < 2):
                        dve.wait_ge(actT_ps, t - 1)
                    dve.tensor_tensor(act_s[p][:, :], g1[p][:, :], up_ps[:, p, 1, :], ALU.mult).then_inc(act_ok, 1)
                if t_in(t - 2):
                    dve.wait_ge(dn_ok, t - 1)
                    if not (isinstance(t, int) and t < 4):
                        dve.wait_ge(ys_out[p], 16 * (g - 1))
                    dve.tensor_copy(ys[p][:, :], dn_ps[:, 0:D]).then_inc(ys_ok, 1)

            expert_schedule(dve, expert)

            dve.wait_ge(h1_back, 16)
            dve.wait_ge(yr_in, 16 * NT)
            with dve.Fori(0, NT) as t:
                x = xn2[:, bass.ds(t, 1), :].rearrange("p o d -> p (o d)")
                dve.scalar_tensor_tensor(x, yr[:, bass.ds(t, 1), :].rearrange("p o d -> p (o d)"),
                                         prob[:, bass.ds(t, 1)], x, ALU.mult, ALU.add).then_inc(fin_ok, 1)


_INS = ["patches", "txt", "convT", "conv_bias", "cls", "pos", "inT", "dw_w", "dw_b", "xpT", "dtT", "dt_b", "a_logs",
        "d_skip", "outT", "router_w", "router_b", "w1", "w2", "w3"]


def kernel(x, txt, L0_tok_conv_w, L0_tok_conv_b, L0_tok_cls_token, L0_tok_pos_emb, L0_attn_in_proj_w, L0_attn_conv_w,
           L0_attn_conv_b, L0_attn_x_proj_w, L0_attn_dt_proj_w, L0_attn_dt_proj_b, L0_attn_A_logs, L0_attn_Ds,
           L0_attn_out_proj_w, L0_ffn_router_w, L0_ffn_router_b, L0_ffn_w1, L0_ffn_w2, L0_ffn_w3):
    import numpy as np
    import concourse.bacc as bacc
    from concourse.bass_utils import run_bass_kernel_spmd

    B, C, H, W = x.shape
    D, _, P, _ = L0_tok_conv_w.shape
    n = H // P
    DH, J = D // 2, L0_attn_out_proj_w.shape[1] // 128
    R = L0_attn_dt_proj_w.shape[2]
    S = L0_attn_A_logs.shape[1]
    E, _, HID = L0_ffn_w1.shape
    f = np.float32
    v = np.asarray(x).reshape(B, C, n, P, n, P).transpose(0, 1, 3, 5, 2, 4).reshape(B, C * P * P // 128, 128, n * n)
    patches = np.zeros((B, 128, C * P * P // 128, n * n + 1), f)
    patches[:, :, :, 1:] = v.transpose(0, 2, 1, 3)
    xw = np.asarray(L0_attn_x_proj_w)
    rows = [xw[k, R:] for k in range(2) for _ in range(3)] + [xw[0, :R], np.zeros((64 - R, xw.shape[2]), f), xw[1, :R]]
    xpT = np.concatenate(rows).T.reshape(J, 128, -1).transpose(1, 0, 2)
    dtw = np.asarray(L0_attn_dt_proj_w)
    dtT = np.concatenate([dtw[0].T, np.zeros((64 - R, J * 128), f), dtw[1].T])

    def by_block(a, *rest):
        return np.asarray(a).reshape(-1, 128, *rest).transpose(1, 0, *range(2, 2 + len(rest)))

    arrays = {
        "patches": patches,
        "txt": np.asarray(txt),
        "convT": np.asarray(L0_tok_conv_w).reshape(D, -1, 128).transpose(2, 1, 0),
        "conv_bias": np.broadcast_to(np.asarray(L0_tok_conv_b), (128, D)),
        "cls": np.asarray(L0_tok_cls_token)[0],
        "pos": np.asarray(L0_tok_pos_emb)[0],
        "inT": np.asarray(L0_attn_in_proj_w).T.reshape(2, DH, -1).transpose(1, 0, 2),
        "dw_w": by_block(L0_attn_conv_w, 3),
        "dw_b": by_block(L0_attn_conv_b),
        "xpT": xpT,
        "dtT": dtT,
        "dt_b": by_block(L0_attn_dt_proj_b),
        "a_logs": by_block(L0_attn_A_logs, S),
        "d_skip": by_block(L0_attn_Ds),
        "outT": by_block(np.asarray(L0_attn_out_proj_w).T, D),
        "router_w": np.asarray(L0_ffn_router_w).reshape(2, DH, E).transpose(1, 0, 2),
        "router_b": np.broadcast_to(np.asarray(L0_ffn_router_b), (128, E)),
        "w1": np.asarray(L0_ffn_w1).reshape(E, 2, DH, HID).transpose(2, 1, 0, 3),
        "w2": np.asarray(L0_ffn_w2).reshape(E, 2, DH, HID).transpose(2, 1, 0, 3),
        "w3": np.asarray(L0_ffn_w3).reshape(E, HID // 128, 128, D).transpose(2, 1, 0, 3),
    }
    nc = bacc.Bacc("TRN2", target_bir_lowering=False, num_devices=1)
    feeds, args = {}, []
    for name in _INS:
        a = np.ascontiguousarray(arrays[name])
        feeds[f"in_{name}"] = a
        args.append(nc.dram_tensor(f"in_{name}", a.shape, mybir.dt.from_np(a.dtype), kind="ExternalInput").ap())
    L = n * n + 1 + txt.shape[1]
    out = nc.dram_tensor("out", (B * L, D), mybir.dt.float32, kind="ExternalOutput").ap()
    early_fusion_kernel(nc, *args, out)
    r = run_bass_kernel_spmd(nc, [feeds], core_ids=[0])
    return r.results[0]["out"].reshape(B, L, D)
```

```python
import concourse.bass as bass
from concourse import mybir
from contextlib import ExitStack


def early_fusion_kernel(nc: bass.Bass, patches, txt, convT, conv_bias, cls, pos, inT, dw_w, dw_b, xpT, dtT, dt_b,
                        a_logs, d_skip, outT, router_w, router_b, w1, w2, w3, out):
    f32, bf16, u32, i32 = mybir.dt.float32, mybir.dt.bfloat16, mybir.dt.uint32, mybir.dt.int32
    ALU, ACT, AX = mybir.AluOpType, mybir.ActivationFunctionType, mybir.AxisListType

    B = patches.shape[0]
    KC = patches.shape[2]
    NPOS = patches.shape[3]
    NTXT = txt.shape[1]
    D = txt.shape[2]
    DH = D // 2
    L = NPOS + NTXT
    J = outT.shape[1]
    NS = a_logs.shape[2]
    RANK = (dtT.shape[0] - 64) if dtT.shape[0] > 64 else dtT.shape[0]
    E = router_w.shape[2]
    HID = w1.shape[3]
    HC = HID // 128
    T = B * L
    EPS = 1e-5
    ROWS = [(NPOS + 1) // 2, NPOS // 2, NTXT]
    OFF = [0, ROWS[0], NPOS]
    R0 = ROWS[0]

    NT = (T + 127) // 128
    NX = (NT * 128 - E) // 128 + E
    hn_d = nc.dram_tensor("ln1_T", (B, DH, 2 * L), f32, kind="Internal").ap()
    h0_d = nc.dram_tensor("h0", (B, R0, 3 * D), f32, kind="Internal").ap()
    h1_d = nc.dram_tensor("h1", (NT * 128, D), f32, kind="Internal").ap()
    sorted_x = nc.dram_tensor("sorted_x", (NX * 128, D + 1), f32, kind="Internal").ap()
    token_y = nc.dram_tensor("token_y", (NT * 128 + 128, D), bf16, kind="Internal").ap()

    top = ExitStack()
    with top:
        def sem(name):
            return top.enter_context(nc.semaphore(name))

        def sb(stack, name, shape, dt=f32):
            return stack.enter_context(nc.sbuf_tensor(name, shape, dt))

        def ps(stack, name, shape):
            return stack.enter_context(nc.psum_tensor(name, shape, f32))

        ident = sb(top, "ident", [128, 128])
        zero_s = sb(top, "zero_s", [128, D + 1])

        s2c = ExitStack()
        inT_s = sb(s2c, "inT_s", [DH, 2, 2 * J * 128])
        xpT_s = sb(s2c, "xpT_s", [128, J, xpT.shape[2]])
        dtT_s = sb(s2c, "dtT_s", [dtT.shape[0], J * 128])
        outT_s = sb(s2c, "outT_s", [128, J, D])
        dww = sb(s2c, "dww", [128, J, 3])
        dwb = sb(s2c, "dwb", [128, J])
        dtb = sb(s2c, "dtb", [128, 2 * J])
        alog = sb(s2c, "alog", [128, 2 * J, NS])
        a_neg = sb(s2c, "a_neg", [128, 2 * J, NS])
        dsk = sb(s2c, "dsk", [128, 2 * J])
        dsum = sb(s2c, "dsum", [128, J])
        diag_d = sb(s2c, "diag_d", [128, J, 128])
        sel = sb(s2c, "sel", [96, 2 * NS, 128], bf16)
        hx = [sb(s2c, f"hx{p}", [DH, 2, L]) for p in range(2)]

        s1 = ExitStack()
        convT_s = sb(s1, "convT_s", [128, KC, D])
        posb = sb(s1, "posb", [R0, 2, D])
        emb_bias = sb(s1, "emb_bias", [R0, 2, D])
        xt = [sb(s1, f"xt{p}", [128, KC, NPOS]) for p in range(2)]
        h0 = [sb(s1, f"h0_{p}", [R0, 3, D]) for p in range(2)]
        xn = [sb(s1, f"xn{p}", [R0, 3, D]) for p in range(2)]
        hnT = [sb(s1, f"hnT{p}", [DH, 2, L]) for p in range(2)]
        bst = [sb(s1, f"bst{p}", [R0, 3, 6]) for p in range(2)]
        sd = [sb(s1, f"sd{p}", [R0, 6, 3]) for p in range(2)]
        rt = [sb(s1, f"rt{p}", [R0, 3]) for p in range(2)]
        ps1 = ExitStack()
        emb_ps = ps(ps1, "emb_ps", [128, 2, 2, 512])
        tr_ps = ps(ps1, "tr_ps", [128, 2, 2, 512])
        s1.close()
        ps1.close()

        HN = NS // 2
        PAIRS = HN // 2
        DP = PAIRS - 1
        ND = J * DP
        RING = 9
        s2 = ExitStack()
        hres = [sb(s2, f"hres{p}", [R0, 3, D]) for p in range(2)]
        xraw = sb(s2, "xraw", [128, J, L])
        xc = sb(s2, "xc", [128, J, L])
        u_s = sb(s2, "u_s", [128, J, L])
        z_s = [sb(s2, f"z_s{p}", [128, J, L]) for p in range(2)]
        dt_in = sb(s2, "dt_in", [dtT.shape[0], L])
        bcf = sb(s2, "bcf", [96, 2, L])
        rest1 = sb(s2, "rest1", [96, L])
        mid = sb(s2, "mid", [96, L], bf16)
        bcs = [sb(s2, f"bcs{p}", [96, 2, L], bf16) for p in range(2)]
        absx = sb(s2, "absx", [128, J, L])
        relx = sb(s2, "relx", [128, J, L])
        delta = sb(s2, "delta", [128, 2, J, L])
        du = [sb(s2, f"du{p}", [128, 2, J, L]) for p in range(2)]
        dA = [sb(s2, f"dA{v}", [128, J, HN, L + 1]) for v in range(2)]
        h_s = sb(s2, "h_s", [128, J, HN, L + 1])
        hc = sb(s2, "hc", [128, RING, 2, L])
        gb = sb(s2, "gb", [128, 2, L])
        gc = sb(s2, "gc", [128, 2, L])
        hcg = sb(s2, "hcg", [128, J, 2, L])
        yg = sb(s2, "yg", [128, J, L])
        ps2 = ExitStack()
        bc_ps = ps(ps2, "bc_ps", [128, 2, 2, 512])
        y_ps = ps(ps2, "y_ps", [128, J, 512])
        misc = ps(ps2, "misc", [128, 512])
        s2.close()
        s2c.close()
        ps2.close()

        s3 = ExitStack()
        w1_s = sb(s3, "w1_s", [DH, 2, E, HID])
        w2_s = sb(s3, "w2_s", [DH, 2, E, HID])
        w3_s = sb(s3, "w3_s", [128, HC, E, D])
        xn2 = sb(s3, "xn2", [128, NT, D + 1])
        bst2 = sb(s3, "bst2", [128, NT, 6])
        stat = sb(s3, "stat", [128, 6, NT])
        root = sb(s3, "root", [128, NT])
        rw_s = sb(s3, "rw_s", [DH, 2, E])
        rb_s = sb(s3, "rb_s", [128, E])
        x2T = [sb(s3, f"x2T{p}", [DH, 2, 2, 128]) for p in range(2)]
        lg = sb(s3, "lg", [128, NT, E])
        lt = sb(s3, "lt", [128, NT, E])
        lmax = sb(s3, "lmax", [128, NT])
        best = sb(s3, "best", [128, NT])
        prob = sb(s3, "prob", [128, NT])
        onehot = sb(s3, "onehot", [128, NT, E])
        tri = sb(s3, "tri", [128, 128])
        ones = sb(s3, "ones", [128, 128])
        rank_e = sb(s3, "rank_e", [128, NT, E])
        cnt = sb(s3, "cnt", [128, E, NT])
        cum = sb(s3, "cum", [128, E, NT + 1])
        tot_i = sb(s3, "tot_i", [128, E], i32)
        pad_f = sb(s3, "pad_f", [128, E])
        ends = sb(s3, "ends", [128, E + 1])
        prio = sb(s3, "prio", [128, E])
        slot_f = sb(s3, "slot_f", [128, NT])
        slot_u = sb(s3, "slot_u", [128, NT], u32)
        start_f = sb(s3, "start_f", [1, NX])
        texp = sb(s3, "texp", [1, NX])
        texp_i = sb(s3, "texp_i", [1, NX], i32)
        xs = [sb(s3, f"xs{p}", [128, D + 1]) for p in range(2)]
        hold = [sb(s3, f"hold{p}", [128, 1]) for p in range(2)]
        later = [sb(s3, f"later{p}", [128, 1]) for p in range(2)]
        tok_u = [sb(s3, f"tok_u{p}", [128, 1], u32) for p in range(2)]
        xsT = [sb(s3, f"xsT{p}", [DH, 2, 128]) for p in range(2)]
        g1 = [sb(s3, f"g1_{p}", [128, HID]) for p in range(2)]
        act_s = [sb(s3, f"act_s{p}", [128, HID]) for p in range(2)]
        actT = [sb(s3, f"actT{p}", [128, HC, 128]) for p in range(2)]
        ys = [sb(s3, f"ys{p}", [128, D], bf16) for p in range(2)]
        yr = sb(s3, "yr", [128, NT, D], bf16)
        s3.close()
        ps3 = ExitStack()
        tr3 = ps(ps3, "tr3", [128, 2, 512])
        up_ps = ps(ps3, "up_ps", [128, 2, 2, 512])
        at_ps = ps(ps3, "at_ps", [128, 512])
        dn_ps = ps(ps3, "dn_ps", [128, 512])
        ps3.close()
        TB = 512 // E
        NB = (NT + TB - 1) // TB
        lg_ps = up_ps[:, 0, :, :]
        cnt_ps = [at_ps, dn_ps]
        assert NB <= 2 and NT <= 128

        w1_in = sem("w1_in")
        w2_in = sem("w2_in")
        w3_in = sem("w3_in")
        gp_set = sem("gp_set")
        clear1 = sem("clear1")
        posb_ok = sem("posb_ok")
        xt_in = [sem(f"xt_in{p}") for p in range(2)]
        txt_in = [sem(f"txt_in{p}") for p in range(2)]
        emb_mm = sem("emb_mm")
        h0_ok = sem("h0_ok")
        st_chain = sem("st_chain")
        sqrt_ok = sem("sqrt_ok")
        xn_ok = sem("xn_ok")
        tr_ok = sem("tr_ok")
        hnT_ok = sem("hnT_ok")
        hn_out = [sem(f"hn_out{p}") for p in range(2)]
        h0_out = [sem(f"h0_out{p}") for p in range(2)]

        set2 = sem("set2")
        pads = sem("pads")
        hx_in = [sem(f"hx_in{p}") for p in range(2)]
        hres_in = [sem(f"hres_in{p}") for p in range(2)]
        misc_full = sem("misc_full")
        misc_free = sem("misc_free")
        xc_left = sem("xc_left")
        xc_ok = sem("xc_ok")
        u_ok = sem("u_ok")
        sp_exp = sem("sp_exp")
        sp_ln = sem("sp_ln")
        bcf_ok = sem("bcf_ok")
        split = sem("split")
        delta_ok = sem("delta_ok")
        du_ok = sem("du_ok")
        bc_full = sem("bc_full")
        g_full = sem("g_full")
        g_ready = sem("g_ready")
        dbu = sem("dbu")
        dbu_g = sem("dbu_g")
        da_ok = sem("da_ok")
        scan_ok = sem("scan_ok")
        hc_full = sem("hc_full")
        hc_free = sem("hc_free")
        hcg_full = sem("hcg_full")
        hcg_free = sem("hcg_free")
        skip_ok = sem("skip_ok")
        gated = sem("gated")
        h1_out = [sem(f"h1_out{p}") for p in range(2)]

        zero_ok = sem("zero_ok")
        zero_out = sem("zero_out")
        ROLL = next(r for r in (3, 2, 1) if NT % r == 0)
        parts = [0, NT // ROLL // 4, NT // ROLL // 2, NT // ROLL]
        H1_PARTS = [(a * ROLL, b * ROLL) for a, b in zip(parts, parts[1:])]
        NM = (NT + 1) // 2
        h1_in = [sem(f"h1_in{n}") for n in range(len(H1_PARTS))]
        wr_in = sem("wr_in")
        ln2 = sem("ln2")
        sqrt2 = sem("sqrt2")
        xn2_ok = sem("xn2_ok")
        tr2_ok = sem("tr2_ok")
        x2T_ok = sem("x2T_ok")
        lg_ok = sem("lg_ok")
        route = sem("route")
        rexp = sem("rexp")
        rank_ok = sem("rank_ok")
        scat = sem("scat")
        xs_in = [sem(f"xs_in{p}") for p in range(2)]
        xsT_ps = sem("xsT_ps")
        xsT_ok = sem("xsT_ok")
        up_ok = sem("up_ok")
        g1_ok = sem("g1_ok")
        act_ok = sem("act_ok")
        actT_ps = sem("actT_ps")
        actT_ok = sem("actT_ok")
        dn_ok = sem("dn_ok")
        ys_ok = sem("ys_ok")
        ys_out = sem("ys_out")
        h1_back = sem("h1_back")
        hold_ok = sem("hold_ok")
        later_ok = sem("later_ok")
        tok_ok = sem("tok_ok")
        y_parts = range(0, NT, 8 * ROLL)
        yr_in = [sem(f"yr_in{n}") for n in range(len(y_parts))]
        fin_ok = sem("fin_ok")
        fin_out = sem("fin_out")

        LN2_VAR = NT + 7
        PADDED = NT * 128 > T
        GROUP = 4 * ROLL
        W1_DMAS = 6
        W2_DMAS = 9
        W3_DMAS = 3
        ROUTE_LT = NB + 3
        ROUTE_HOT = NB + 5
        ROUTE_ALL = ROUTE_HOT + 2 + 2 * NB + 1 + E + 3 + 2 + 5 + E + 1

        block = top.enter_context(nc.Block())

        USES = [(0, "b", "x", 0, 0), (0, "d", "x", 1, 0), (0, "e", "x", 2, 0),
                (1, "a", "o", 0, 0), (1, "b", "o", 1, 0), (1, "c", "o", 2, 0), (1, "d", "z", 0, 0), (1, "e", "z", 1, 0),
                (2, "a", "dt", 0, 0), (2, "b", "bc", 0, 0), (2, "c", "bc", 0, 1),
                (2, "d", "p", 0, 0), (2, "e", "p", 1, 0), (3, "a", "p", 2, 0), (3, "b", "z", 2, 0),
                (3, "c", "p", 0, 1), (3, "e", "p", 1, 1), (3, "e", "p", 2, 1)]
        O_LAST, BC0, Z_LAST = 5, 9, 14
        SUMS = [("d", 0), ("g", 0), ("d", 1), ("d", 2), ("g", 1), ("d", 3), ("g", 2)]
        SUMS += [("d", n) for n in range(4, ND)]
        NO = 3
        NF = len(USES) - NO

        def use_count(i, n):
            o_before = sum(1 for u in USES[:n] if u[2] == "o")
            if i is None:
                return n - o_before
            if is_first(i):
                return NF + n - o_before
            if is_last(i):
                return NF + len(USES) * i - NO + o_before
            if isinstance(i, int) and i == B:
                return NF + len(USES) * (B - 1) + n
            return NF + len(USES) * i - NO + n

        def uses_at(i, unit, place):
            found = []
            for n, (a, b, kind, j, k) in enumerate(USES):
                if (a, b) == (unit, place) and not (is_first(i) if kind == "o" else is_last(i)):
                    found.append((n, kind, j, k))
            return found

        def is_first(i):
            return isinstance(i, int) and i == 0

        def is_last(i):
            return isinstance(i, int) and i == B - 1

        def front_uses():
            return [(n, kind, j, k) for n, (_, _, kind, j, k) in enumerate(USES) if kind != "o"]

        def t_of(t, n):
            return not isinstance(t, int) or 0 <= t < n

        def t_in(t):
            return t_of(t, NX)

        def in_pairs(eng, n, step):
            for t in range(2):
                step(t, t)
            with eng.Fori(1, n // 2) as g:
                for p in range(2):
                    step(2 * g + p, p)
            if n % 2:
                step(n - 1, 0)

        def expert_schedule(eng, step):
            for t in range(4):
                step(t, t % 2, t // 2)
            last = NX // 2 - 1
            with eng.Fori(2, last) as g:
                for p in range(2):
                    step(2 * g + p, p, g)
            for t in range(2 * last, NX + 2):
                step(t, t % 2, t // 2)

        @block.sync
        def _(sp):
            def load_xt(i, p):
                sp.dma_start(xt[p][:, :, :], patches[i]).then_inc(xt_in[p], 16)

            def load_txt(i, p):
                sp.dma_start(h0[p][0:NTXT, 2, :], txt[i]).then_inc(txt_in[p], 16)

            sp.dma_start(convT_s[:, :, :], convT).then_inc(w1_in, 16)
            load_xt(0, 0)
            sp.dma_start(posb[:, 0, :], pos[0:R0]).then_inc(w1_in, 16)
            sp.dma_start(posb[0:ROWS[1], 1, :], pos[R0:NPOS]).then_inc(w1_in, 16)
            sp.dma_start(emb_bias[1:R0, 0, :], conv_bias[0:R0 - 1]).then_inc(w1_in, 16)
            sp.dma_start(emb_bias[0:1, 0, :], cls).then_inc(w1_in, 16)
            sp.dma_start(emb_bias[0:ROWS[1], 1, :], conv_bias[0:ROWS[1]]).then_inc(w1_in, 16)
            load_xt(1, 1)
            sp.wait_ge(clear1, 4)
            load_txt(0, 0)
            load_txt(1, 1)
            for dst, src in ((inT_s, inT), (xpT_s, xpT), (dtT_s, dtT), (outT_s, outT), (dww, dw_w), (dwb, dw_b),
                             (dtb, dt_b), (alog, a_logs), (dsk, d_skip)):
                d = dst[tuple(slice(None) for _ in dst.shape)]
                sp.dma_start(d, src).then_inc(w2_in, 16)

            def store1(i, p, g):
                sp.wait_ge(xn_ok, i + 1)
                sp.dma_start(h0_d[i], h0[p][:, :, :].rearrange("r t d -> r (t d)")).then_inc(h0_out[p], 16)
                sp.wait_ge(hnT_ok, i + 1)
                sp.dma_start(hn_d[i], hnT[p][:, :, :].rearrange("r t d -> r (t d)")).then_inc(hn_out[p], 16)

            with sp.Fori(0, B // 2 - 1) as g:
                for p in range(2):
                    i = 2 * g + p
                    sp.wait_ge(emb_mm, i + 1)
                    load_xt(i + 2, p)
                    store1(i, p, g)
                    sp.wait_ge(h0_out[p], 16 * g + 16)
                    load_txt(i + 2, p)
            for p in range(2):
                store1(B - 2 + p, p, B // 2 - 1)

            def load_hx(i, p):
                sp.dma_start(hx[p][:, :, :].rearrange("r t d -> r (t d)"), hn_d[i]).then_inc(hx_in[p], 16)

            sp.wait_ge(hn_out[0], 16 * (B // 2))
            load_hx(0, 0)
            for p in range(2):
                sp.wait_ge(hn_out[p], 16 * (B // 2))
                sp.wait_ge(h0_out[p], 16 * (B // 2))

            sp.wait_ge(zero_ok, 2)
            sp.dma_start(sorted_x.rearrange("(t p) d -> p t d", p=128),
                         zero_s[:, :].unsqueeze(1).to_broadcast([128, NX, D + 1])).then_inc(zero_out, 16)
            if PADDED:
                sp.dma_start(h1_d[T:NT * 128], zero_s[0:NT * 128 - T, 0:D]).then_inc(zero_out, 16)

            def load_res(i, p):
                sp.dma_start(hres[p][:, :, :].rearrange("r t d -> r (t d)"), h0_d[i]).then_inc(hres_in[p], 16)

            def store_h1(i, p, count):
                sp.wait_ge(misc_free, count)
                for t in range(3):
                    sp.dma_start(h1_d[bass.ds(L * i + OFF[t], ROWS[t])], hres[p][0:ROWS[t], t, :])\
                      .then_inc(h1_out[p], 16)

            def body(i, p, g):
                if not is_last(i):
                    if not is_first(i):
                        first = isinstance(i, int) and i == 1
                        sp.wait_ge(misc_full, use_count(None if first else i - 2, Z_LAST) + 1)
                    load_hx(i + 1, 1 - p)
                if not (isinstance(i, int) and i < 2):
                    sp.wait_ge(h1_out[p], 48 * g)
                load_res(i, p)
                if not is_first(i):
                    store_h1(i - 1, 1 - p, use_count(i, O_LAST) + 1)

            body(0, 0, 0)
            body(1, 1, 0)
            body(2, 0, 1)
            if B > 4:
                with sp.Fori(1, B // 2 - 1) as g:
                    body(2 * g + 1, 1, g)
                    body(2 * g + 2, 0, g + 1)
            body(B - 1, 1, B // 2 - 1)
            store_h1(B - 1, 1, use_count(B, NO))

            for p in range(2):
                sp.wait_ge(h1_out[p], 48 * (B // 2))
            sp.wait_ge(misc_free, use_count(B, NO))
            sp.wait_ge(zero_out, 32 if PADDED else 16)
            for dst, src in ((rw_s, router_w), (rb_s, router_b)):
                d = dst[tuple(slice(None) for _ in dst.shape)]
                sp.dma_start(d, src).then_inc(wr_in, 16)
            h1_v = h1_d.rearrange("(p t) d -> p t d", p=128)
            for n, (a, b) in enumerate(H1_PARTS):
                sp.dma_start(xn2[:, a:b, 0:D], h1_v[:, a:b, :]).then_inc(h1_in[n], 16)
            for dst, src in ((w1_s, w1), (w2_s, w2), (w3_s, w3)):
                d = dst[tuple(slice(None) for _ in dst.shape)]
                sp.dma_start(d, src).then_inc(w3_in, 16)

            def load_xs(t, p):
                sp.dma_start(xs[p][:, :], sorted_x[bass.ds(128 * t, 128)]).then_inc(xs_in[p], 16)

            sp.wait_ge(scat, 16 * NT)
            load_xs(0, 0)
            load_xs(1, 1)
            def next_xs(t, p):
                sp.wait_ge(xsT_ps, t - 1)
                sp.wait_ge(hold_ok, t - 1)
                load_xs(t, p)

            BACK = NT // ROLL + 1
            with sp.Fori(1, BACK) as g:
                for p in range(2):
                    next_xs(2 * g + p, p)
                sp.dma_start(xn2[:, bass.ds(ROLL * (g - 1), ROLL), 0:D], h1_v[:, bass.ds(ROLL * (g - 1), ROLL), :])\
                  .then_inc(h1_back, 16)
            with sp.Fori(BACK, NX // 2) as g:
                for p in range(2):
                    next_xs(2 * g + p, p)
            if NX % 2:
                next_xs(NX - 1, 0)
            sp.wait_ge(ys_out, 16 * NX)
            ty_v = token_y[0:NT * 128].rearrange("(p t) d -> p t d", p=128)
            for n, a in enumerate(y_parts):
                b = min(a + 8 * ROLL, NT)
                sp.dma_start(yr[:, a:b, :], ty_v[:, a:b, :]).then_inc(yr_in[n], 16)
            full = T // NT
            stores = 0
            for a in range(0, NT, GROUP):
                b = min(a + GROUP, NT)
                sp.wait_ge(fin_ok, b)
                sp.dma_start(out[0:full * NT].rearrange("(p t) d -> p t d", t=NT)[:, a:b, :],
                             xn2[0:full, a:b, 0:D]).then_inc(fin_out, 16)
                stores += 1
                c = min(b, T % NT)
                if c > a:
                    sp.dma_start(out[full * NT + a:full * NT + c], xn2[full:full + 1, a:c, 0:D]).then_inc(fin_out, 16)
                    stores += 1
            sp.wait_ge(fin_out, 16 * stores)

        @block.gpsimd
        def _(gp):
            gp.memset(zero_s[:, 0:D], 0.0).then_inc(zero_ok, 1)
            gp.iota(zero_s[:, D:D + 1], pattern=[[1, 1]], base=NT * 128, channel_multiplier=1,
                    allow_small_or_imprecise_dtypes=True).then_inc(zero_ok, 1)
            gp.memset(ident[:, :], 0.0).then_inc(gp_set, 1)
            gp.wait_ge(gp_set, 1)
            gp.affine_select(out=ident[:, :], in_=ident[:, :], compare_op=ALU.not_equal, fill=1.0, base=0,
                             pattern=[[-1, 128]], channel_multiplier=1).then_inc(gp_set, 1)
            gp.memset(sel[:, :, :], 0.0).then_inc(gp_set, 1)
            for part in range(3):
                gp.wait_ge(gp_set, 3 + part)
                gp.affine_select(out=sel[:, :, :], in_=sel[:, :, :], compare_op=ALU.not_equal, fill=1.0,
                                 base=-32 * part, pattern=[[-1, 2 * NS], [0, 128]], channel_multiplier=1)\
                  .then_inc(gp_set, 1)
            gp.wait_ge(hnT_ok, B)
            gp.wait_ge(xn_ok, B)
            for p in range(2):
                gp.wait_ge(hn_out[p], 16 * (B // 2))
                gp.wait_ge(h0_out[p], 16 * (B // 2))
            for buf in (dA[0], dA[1], h_s):
                gp.memset(buf[:, :, :, 0:1], 0.0).then_inc(pads, 1)

            def split_bc(i, k, p):
                base = 4 * (2 * (0 if i is None else i + 1) + k)
                if i is not None and k == 0:
                    gp.wait_ge(dbu_g, J * (4 * i + 4))
                gp.wait_ge(misc_free, use_count(i, BC0 + k) + 1)
                hi, lo = bcs[p][32:64, k, :], bcs[p][64:96, k, :]
                gp.tensor_tensor(rest1[64:96, :], bcf[64:96, k, :], lo, ALU.subtract).then_inc(split, 1)
                gp.tensor_tensor(mid[64:96, :], bcf[64:96, k, :], lo, ALU.subtract).then_inc(split, 1)
                gp.tensor_tensor(hi, bcf[32:64, k, :], hi, ALU.subtract).then_inc(split, 1)
                gp.wait_ge(split, base + 2)
                gp.tensor_tensor(lo, rest1[64:96, :], mid[64:96, :], ALU.subtract).then_inc(split, 1)
                gp.wait_ge(split, base + 4)

            def delta_du(i, k, p):
                gp.wait_ge(sp_ln, 2 * i + k + 1)
                if not is_first(i):
                    gp.wait_ge(da_ok, 3 * (4 * (i - 1) + 2 * k + 2))
                gp.tensor_tensor(delta[:, k, :, :], relx[:, :, :], absx[:, :, :], ALU.add).then_inc(delta_ok, 1)
                gp.wait_ge(delta_ok, 2 * i + k + 1)
                gp.wait_ge(u_ok, i + 1)
                if not (isinstance(i, int) and i < 2):
                    gp.wait_ge(dbu, ND * 4 * (i - 1))
                    gp.wait_ge(dbu_g, J * 4 * (i - 1))
                gp.tensor_tensor(du[p][:, k, :, :], delta[:, k, :, :], u_s[:, :, :], ALU.mult).then_inc(du_ok, 1)

            def times_b(i, unit, p):
                k, U = unit // 2, 4 * i + unit
                gp.wait_ge(g_ready, 2 * U + 1)
                gp.wait_ge(du_ok, 2 * i + k + 1)
                for j in range(J):
                    if not (isinstance(U, int) and U == 0):
                        gp.wait_ge(hcg_full, J * (U - 1) + j + 1)
                    gp.tensor_tensor(h_s[:, j, 0:2, 1:L + 1], gb[:, :, :],
                                     du[p][:, k, j:j + 1, :].to_broadcast([128, 2, L]), ALU.mult).then_inc(dbu_g, 1)

            def times_c(i, unit):
                U = 4 * i + unit
                gp.wait_ge(g_ready, 2 * U + 2)
                for j in range(J):
                    gp.wait_ge(scan_ok, J * U + j + 1)
                    if not (isinstance(U, int) and U == 0):
                        gp.wait_ge(hcg_free, J * (U - 1) + j + 1)
                    gp.tensor_tensor(hcg[:, j, :, :], h_s[:, j, 0:2, 1:L + 1], gc[:, :, :], ALU.mult)\
                      .then_inc(hcg_full, 1)

            def body(i, p):
                for unit in range(4):
                    if unit == 3 and not is_last(i):
                        delta_du(i + 1, 0, 1 - p)
                    times_c(i, unit)
                    if unit < 3:
                        times_b(i, unit + 1, p)
                    elif not is_last(i):
                        times_b(i + 1, 0, 1 - p)
                        delta_du(i + 1, 1, 1 - p)
                    if unit == 2 and not is_last(i):
                        for k in range(2):
                            split_bc(i, k, 1 - p)

            for k in range(2):
                split_bc(None, k, 0)
            delta_du(0, 0, 0)
            times_b(0, 0, 0)
            delta_du(0, 1, 0)
            body(0, 0)
            if B > 2:
                with gp.Fori(0, B // 2 - 1) as g:
                    body(2 * g + 1, 1)
                    body(2 * g + 2, 0)
            body(B - 1, 1)

            gp.wait_ge(h1_in[0], 16)
            gp.memset(ones[:, :], 1.0).then_inc(gp_set, 1)
            gp.wait_ge(gp_set, 7)
            gp.affine_select(out=tri[:, :], in_=ones[:, :], compare_op=ALU.is_gt, fill=0.0, base=0,
                             pattern=[[1, 128]], channel_multiplier=-1).then_inc(gp_set, 1)
            gp.iota(start_f[:, :], pattern=[[128, NX]], base=0, channel_multiplier=0,
                    allow_small_or_imprecise_dtypes=True).then_inc(gp_set, 1)
            gp.iota(prio[:, :], pattern=[[-1, E]], base=E, channel_multiplier=0,
                    allow_small_or_imprecise_dtypes=True).then_inc(gp_set, 1)
            gp.iota(xn2[:, :, D:D + 1], pattern=[[1, NT], [1, 1]], base=0, channel_multiplier=NT,
                    allow_small_or_imprecise_dtypes=True).then_inc(gp_set, 1)
            gp.wait_ge(gp_set, 11)
            gp.wait_ge(route, ROUTE_ALL)
            for t in range(NT):
                gp.indirect_dma_start(sorted_x, bass.IndirectOffsetOnAxis(ap=slot_u[:, t:t + 1], axis=0),
                                      xn2[:, t, :], None).then_inc(scat, 16)

            def store_ys(t, p):
                gp.wait_ge(ys_ok, t + 1)
                if not (isinstance(t, int) and t < 1):
                    gp.wait_ge(ys_out, 16 * t)
                gp.indirect_dma_start(token_y, bass.IndirectOffsetOnAxis(ap=tok_u[p][:, 0:1], axis=0),
                                      ys[p][:, :], None).then_inc(ys_out, 16)

            for t in range(NX):
                store_ys(t, t % 2)

        @block.scalar
        def _(act):
            def ln1(i, p, g):
                act.wait_ge(st_chain, 11 * i + 10)
                act.activation(rt[p][:, :], sd[p][:, 4, :], ACT.Sqrt).then_inc(sqrt_ok, 1)
                act.wait_ge(tr_ok, i + 1)
                if not (isinstance(i, int) and i < 2):
                    act.wait_ge(hn_out[p], 16 * g)
                act.activation(hnT[p][:, :, :], tr_ps[0:DH, p, :, 0:L], ACT.Copy).then_inc(hnT_ok, 1)

            ln1(0, 0, 0)
            ln1(1, 1, 0)
            act.wait_ge(w2_in, 16 * W2_DMAS)
            act.activation(a_neg[:, :, :], alog[:, :, :], ACT.Exp).then_inc(set2, 1)
            with act.Fori(1, B // 2) as g:
                for p in range(2):
                    ln1(2 * g + p, p, g)

            for p in range(2):
                act.wait_ge(hn_out[p], 16 * (B // 2))
                act.wait_ge(h0_out[p], 16 * (B // 2))
            act.wait_ge(xn_ok, B)
            act.wait_ge(set2, 3)

            def take(i, n, kind, j, k, p):
                count = use_count(i, n)
                nxt = 0 if i is None else i + 1
                act.wait_ge(misc_full, count + 1)
                if kind == "x":
                    if i is not None:
                        act.wait_ge(u_ok, nxt)
                    act.activation(xc[:, j, :], misc[:, 0:L], ACT.Identity, bias=dwb[:, j:j + 1],
                                   scale=dww[:, j, 1:2])
                    act.activation(xraw[:, j, :], misc[:, 0:L], ACT.Copy).then_inc(misc_free, 1)
                elif kind == "o":
                    act.activation(hres[p][0:ROWS[j], j, :], misc[0:ROWS[j], 0:D], ACT.Copy).then_inc(misc_free, 1)
                elif kind == "z":
                    if j == 0 and i is not None and not is_first(i):
                        act.wait_ge(gated, 3 * i)
                    act.activation(z_s[p][:, j, :], misc[:, 0:L], ACT.Copy).then_inc(misc_free, 1)
                elif kind == "dt":
                    act.activation(dt_in[:, :], misc[0:dtT.shape[0], 0:L], ACT.Copy).then_inc(misc_free, 1)
                elif kind == "bc":
                    if i is not None:
                        act.wait_ge(split, 4 * (2 * (nxt - 1) + k + 1))
                    act.activation(bcf[:, k, :], misc[0:96, 0:L], ACT.Copy).then_inc(bcf_ok, 1)
                    if i is not None and not is_first(i):
                        act.wait_ge(bc_full, 2 * DP * 4 * (nxt - 1))
                        act.wait_ge(g_full, 2 * 4 * (nxt - 1))
                    act.wait_ge(bcf_ok, 2 * nxt + k + 1)
                    act.activation(bcs[p][:, k, :], misc[0:96, 0:L], ACT.Copy).then_inc(misc_free, 1)
                elif kind == "p":
                    if j == 0 and not (i is None and k == 0):
                        act.wait_ge(delta_ok, 2 * nxt + k)
                    b = dtb[:, J * k + j:J * k + j + 1]
                    act.activation(absx[:, j, :], misc[:, 0:L], ACT.Abs, bias=b).then_inc(sp_exp, 1)
                    act.activation(relx[:, j, :], misc[:, 0:L], ACT.Relu, bias=b).then_inc(misc_free, 1)
                    if j == 2:
                        c = 4 * (2 * nxt + k)
                        act.wait_ge(sp_exp, c + 3)
                        act.activation(absx[:, :, :], absx[:, :, :], ACT.Exp, scale=-1.0).then_inc(sp_exp, 1)
                        act.wait_ge(sp_exp, c + 4)
                        act.wait_ge(misc_free, count + 1)
                        act.activation(absx[:, :, :], absx[:, :, :], ACT.Ln, bias=1.0).then_inc(sp_ln, 1)

            def silu(nxt, i):
                act.wait_ge(xc_ok, J * nxt + J)
                if i is not None:
                    act.wait_ge(skip_ok, nxt)
                    act.wait_ge(du_ok, 2 * nxt)
                act.activation(u_s[:, :, :], xc[:, :, :], ACT.Silu).then_inc(u_ok, 1)
                act.preload_act_table_set("natural_log_exp_and_others")

            def exps(i, unit, items):
                k, half = unit // 2, unit % 2
                v = unit % 2
                V = 4 * i + unit
                for m in items:
                    j, n = m // HN, m % HN
                    if n == 0:
                        act.wait_ge(delta_ok, 2 * i + k + 1)
                        if not (isinstance(V, int) and V < 2):
                            act.wait_ge(scan_ok, 3 * (V - 2) + j + 1)
                    a = a_neg[:, J * k + j, half * HN + n:half * HN + n + 1]
                    e = act.activation(dA[v][:, j, n, 1:L + 1], delta[:, k, j, :], ACT.Exp, scale=a)
                    if n == HN - 1:
                        e.then_inc(da_ok, 1)

            def copy_b(U):
                act.wait_ge(g_full, 2 * U + 1)
                if not (isinstance(U, int) and U == 0):
                    act.wait_ge(dbu_g, J * U)
                act.activation(gb[:, :, :], bc_ps[:, 1, :, 0:L], ACT.Copy).then_inc(g_ready, 1)

            def copy_c(U):
                act.wait_ge(g_full, 2 * U + 2)
                if not (isinstance(U, int) and U == 0):
                    act.wait_ge(hcg_full, J * U)
                act.activation(gc[:, :, :], bc_ps[:, 1, :, 0:L], ACT.Copy).then_inc(g_ready, 1)

            def body(i, p):
                for unit in range(4):
                    after, at = (i, unit + 1) if unit < 3 else (i + 1, 0)
                    none = unit == 3 and is_last(i)
                    items = [] if none else list(range(J * HN))

                    def some(n):
                        exps(after, at, items[:n])
                        del items[:n]

                    for place in "abcde":
                        for n, kind, j, k in uses_at(i, unit, place):
                            take(i, n, kind, j, k, 1 - p)
                            if unit < 3:
                                some(2)
                        if place == "a":
                            copy_c(4 * i + unit)
                        if place == "b" and not none:
                            copy_b(4 * i + unit + 1)
                        if place == "c" and unit == 1 and not is_last(i):
                            silu(i + 1, i)
                    some(J * HN)

            for n, kind, j, k in front_uses():
                if kind == "dt":
                    silu(0, None)
                take(None, n, kind, j, k, 0)
            copy_b(0)
            act.wait_ge(pads, 3)
            exps(0, 0, range(J * HN))
            body(0, 0)
            if B > 2:
                with act.Fori(0, B // 2 - 1) as g:
                    body(2 * g + 1, 1)
                    body(2 * g + 2, 0)
            body(B - 1, 1)
            for t in range(NO):
                take(B, t, "o", t, 0, 1)

            act.wait_ge(ln2, LN2_VAR)
            act.activation(root[:, :], stat[:, 4, :], ACT.Sqrt).then_inc(sqrt2, 1)

            def x2T_copy(m, p):
                act.wait_ge(tr2_ok, m + 1)
                if not (isinstance(m, int) and m < 2):
                    act.wait_ge(lg_ok, m - 1)
                n = NT - 2 * m if isinstance(m, int) and 2 * m + 2 > NT else 2
                act.activation(x2T[p][:, 0:n, :, :],
                               tr3[0:DH, p, 0:256 * n].rearrange("p (t a b) -> p t a b", a=2, b=128),
                               ACT.Copy).then_inc(x2T_ok, 1)

            in_pairs(act, NM, x2T_copy)
            act.wait_ge(route, ROUTE_LT)
            act.activation(lt[:, :, :], lt[:, :, :], ACT.Exp).then_inc(rexp, 1)

            def xsT_copy(t, p):
                act.wait_ge(xsT_ps, t + 1)
                if not (isinstance(t, int) and t < 2):
                    act.wait_ge(up_ok, t - 1)
                act.activation(xsT[p][:, :, :], tr3[0:DH, p, 0:256].rearrange("p (a b) -> p a b", a=2),
                               ACT.Copy).then_inc(xsT_ok, 1)

            def expert(t, p, g):
                if t_in(t):
                    act.wait_ge(up_ok, t + 1)
                    if not (isinstance(t, int) and t < 2):
                        act.wait_ge(act_ok, t - 1)
                    act.activation(g1[p][:, :], up_ps[:, p, 0, :], ACT.Silu).then_inc(g1_ok, 1)
                if t_in(t + 2):
                    xsT_copy(t + 2, p)
                if t_in(t - 1):
                    act.wait_ge(actT_ps, t)
                    if not (isinstance(t, int) and t < 3):
                        act.wait_ge(dn_ok, t - 2)
                    act.activation(actT[1 - p][:, :, :], at_ps[:, :].rearrange("p (a b) -> p a b", a=HC), ACT.Copy)\
                       .then_inc(actT_ok, 1)

            xsT_copy(0, 0)
            xsT_copy(1, 1)
            expert_schedule(act, expert)

        @block.tensor
        def _(pe):
            def embed(i, p, g):
                pe.wait_ge(xt_in[p], 16 * g + 16)
                if not (isinstance(i, int) and i < 2):
                    pe.wait_ge(h0_ok, i - 1)
                for t in range(2):
                    for c in range(KC):
                        mm = pe.matmul(emb_ps[0:ROWS[t], p, t, 0:D], xt[p][:, c, OFF[t]:OFF[t] + ROWS[t]],
                                       convT_s[:, c, :], start=(c == 0), stop=(c == KC - 1))
                mm.then_inc(emb_mm, 1)

            def transpose1(i, p):
                pe.wait_ge(xn_ok, i + 1)
                if not (isinstance(i, int) and i < 2):
                    pe.wait_ge(hnT_ok, i - 1)
                for t in range(3):
                    for h in range(2):
                        mm = pe.transpose(tr_ps[0:DH, p, h, OFF[t]:OFF[t] + ROWS[t]],
                                          xn[p][0:ROWS[t], t, DH * h:DH * h + DH], ident[0:ROWS[t], 0:ROWS[t]])
                mm.then_inc(tr_ok, 1)

            pe.wait_ge(w1_in, 16 * W1_DMAS)
            pe.wait_ge(gp_set, 2)
            embed(0, 0, 0)
            embed(1, 1, 0)
            transpose1(0, 0)

            def embed_pair(i, g):
                embed(i + 2, 0, g + 1)
                transpose1(i + 1, 1)
                embed(i + 3, 1, g + 1)
                transpose1(i + 2, 0)

            embed_pair(0, 0)
            with pe.Fori(1, B // 2 - 1) as g:
                embed_pair(2 * g, g)
            transpose1(B - 1, 1)

            def put(i, n, kind, j, k, p, g):
                count = use_count(i, n)
                nxt = 0 if i is None else i + 1
                if not (isinstance(count, int) and count == 0):
                    pe.wait_ge(misc_free, count)
                if kind == "x" or kind == "z":
                    if kind == "x" and j == 0:
                        pe.wait_ge(hx_in[p], 16 * g + 16)
                    c0 = 128 * j + (J * 128 if kind == "z" else 0)
                    for h in range(2):
                        mm = pe.matmul(misc[:, 0:L], inT_s[:, h, c0:c0 + 128], hx[p][:, h, :],
                                       start=(h == 0), stop=(h == 1))
                elif kind == "dt" or kind == "bc":
                    if kind == "dt":
                        pe.wait_ge(u_ok, nxt + 1)
                        c0, m = 192, dtT.shape[0]
                    else:
                        c0, m = 96 * k, 96
                    for jj in range(J):
                        mm = pe.matmul(misc[0:m, 0:L], xpT_s[:, jj, c0:c0 + m], u_s[:, jj, :],
                                       start=(jj == 0), stop=(jj == J - 1))
                elif kind == "p":
                    r = slice(64 * k, 64 * k + RANK)
                    mm = pe.matmul(misc[:, 0:L], dtT_s[r, 128 * j:128 * j + 128], dt_in[r, :], start=True, stop=True)
                elif kind == "o":
                    if j == 0:
                        pe.wait_ge(gated, 3 * i)
                        pe.wait_ge(hres_in[p], 16 * g + 16)
                    for jj in range(J):
                        mm = pe.matmul(misc[0:ROWS[j], 0:D], yg[:, jj, OFF[j]:OFF[j] + ROWS[j]], outT_s[:, jj, :],
                                       start=(jj == 0), stop=False)
                    mm = pe.matmul(misc[0:ROWS[j], 0:D], ident[0:ROWS[j], 0:ROWS[j]], hres[p][0:ROWS[j], j, :],
                                   start=False, stop=True)
                mm.then_inc(misc_full, 1)

            def broadcast(slot, p, unit, c, pair, done):
                k, half = unit // 2, unit % 2
                for m in range(2):
                    n = c * NS + half * HN + 2 * pair + m
                    mm = pe.matmul(bc_ps[:, slot, m, 0:L], sel[:, n, :], bcs[p][:, k, :], start=True, stop=True)
                mm.then_inc(done, 1)

            def add(i, unit, n):
                who, r = SUMS[n]
                U = 4 * i + unit
                if who == "d":
                    pe.wait_ge(hc_full, ND * U + r + 1)
                else:
                    pe.wait_ge(hcg_full, J * U + r + 1)
                for m in range(2):
                    x = hc[:, (ND * unit + r) % RING, m, :] if who == "d" else hcg[:, r, m, :]
                    mm = pe.matmul(y_ps[:, r % J, 0:L], ident[:, :], x, start=False,
                                   stop=unit == 3 and who == "d" and r >= ND - J and m == 1)
                mm.then_inc(hc_free if who == "d" else hcg_free, 1)

            def add_before(i, unit, first, last):
                if not (is_first(i) and unit == 0):
                    for n in range(first, last):
                        add(i if unit else i - 1, (unit - 1) % 4, n)

            def skip(i):
                if not is_first(i):
                    pe.wait_ge(gated, 3 * i)
                for j in range(J):
                    mm = pe.matmul(y_ps[:, j, 0:L], diag_d[:, j, :], u_s[:, j, :], start=True, stop=False)
                mm.then_inc(skip_ok, 1)

            def puts(i, unit, place, p, g):
                for n, kind, j, k in uses_at(i, unit, place):
                    put(i, n, kind, j, k, 1 - p, g + p - 1 if kind == "o" else g + p)
                    if (unit, kind, j) == (0, "x", 2):
                        skip(i)

            def body(i, p, g):
                for unit in range(4):
                    U = 4 * i + unit
                    first = is_first(i) and unit == 0
                    if not first:
                        pe.wait_ge(hc_full, ND * (U - 1) + 2 * J)
                    if unit % 2 == 0:
                        pe.wait_ge(split, 4 * (2 * i + unit // 2 + 1))
                    broadcast(0, p, unit, 0, 1, bc_full)
                    add_before(i, unit, 3, 5)
                    if not first:
                        pe.wait_ge(hc_full, ND * U)
                    else:
                        pe.wait_ge(g_ready, 1)
                    broadcast(1, p, unit, 0, 2, bc_full)
                    add_before(i, unit, 5, 8)
                    pe.wait_ge(dbu, ND * U + J)
                    broadcast(0, p, unit, 0, 3, bc_full)
                    puts(i, unit, "a", p, g)
                    add_before(i, unit, 8, 9)
                    pe.wait_ge(dbu, ND * U + 2 * J)
                    broadcast(1, p, unit, 1, 0, g_full)
                    puts(i, unit, "b", p, g)
                    add_before(i, unit, 9, 10)
                    pe.wait_ge(g_ready, 2 * U + 2)
                    if unit < 3:
                        broadcast(1, p, unit + 1, 0, 0, g_full)
                    elif not is_last(i):
                        pe.wait_ge(split, 4 * (2 * (i + 1) + 1))
                        broadcast(1, 1 - p, 0, 0, 0, g_full)
                    puts(i, unit, "c", p, g)
                    add_before(i, unit, 10, 11)
                    puts(i, unit, "d", p, g)
                    add_before(i, unit, 11, 12)
                    if not (unit == 3 and is_last(i)):
                        pe.wait_ge(g_ready, 2 * U + 3)
                    broadcast(1, p, unit, 1, 1, bc_full)
                    pe.wait_ge(dbu, ND * U + 3 * J)
                    broadcast(0, p, unit, 1, 2, bc_full)
                    if unit == 0 and is_last(i):
                        skip(i)
                    puts(i, unit, "e", p, g)
                    for n in range(2):
                        add(i, unit, n)
                    pe.wait_ge(hc_full, ND * U + J)
                    broadcast(1, p, unit, 1, 3, bc_full)
                    add(i, unit, 2)

            pe.wait_ge(w2_in, 16 * W2_DMAS)
            pe.wait_ge(set2, 3 + J)
            pe.wait_ge(gp_set, 6)
            pe.wait_ge(hnT_ok, B)
            for n, kind, j, k in front_uses():
                put(None, n, kind, j, k, 0, 0)
            pe.wait_ge(split, 4)
            broadcast(1, 0, 0, 0, 0, g_full)
            body(0, 0, 0)
            if B > 2:
                with pe.Fori(0, B // 2 - 1) as g:
                    body(2 * g + 1, 1, g)
                    body(2 * g + 2, 0, g + 1)
            body(B - 1, 1, B // 2 - 1)
            add_before(B, 0, 3, 12)
            for t in range(NO):
                put(B, t, "o", t, 0, 1, B // 2 - 1)

            pe.wait_ge(wr_in, 32)

            def pair2(m, p):
                if m < NM:
                    pe.wait_ge(xn2_ok, min(2 * m + 2, NT))
                    if m >= 2:
                        pe.wait_ge(x2T_ok, m - 1)
                    for t in range(2 * m, min(2 * m + 2, NT)):
                        for h in range(2):
                            c = 256 * (t % 2) + 128 * h
                            mm = pe.transpose(tr3[0:DH, p, c:c + 128], xn2[:, t, DH * h:DH * h + DH], ident[:, :])
                    mm.then_inc(tr2_ok, 1)
                if m > 0:
                    pe.wait_ge(x2T_ok, m)
                    for t in range(2 * m - 2, min(2 * m, NT)):
                        b, c = t // TB, t % TB
                        for h in range(2):
                            mm = pe.matmul(lg_ps[:, b, E * c:E * c + E], x2T[1 - p][:, t % 2, h, :], rw_s[:, h, :],
                                           start=(h == 0), stop=(h == 1), skip_group_check=True)
                    mm.then_inc(lg_ok, 1)

            for m in range(NM + 1):
                pair2(m, m % 2)
            pe.wait_ge(route, ROUTE_HOT)
            pe.wait_ge(gp_set, 10)
            oh = onehot[:, :, :].rearrange("p t e -> p (t e)")
            for ops, out_ps in ((tri, [lg_ps[:, n, :] for n in range(2)]), (ones, [b[:, :] for b in cnt_ps])):
                for n in range(NB):
                    a, b = 512 * n, min(512 * n + 512, NT * E)
                    mm = pe.matmul(out_ps[n][:, 0:b - a], ops[:, :], oh[:, a:b], start=True, stop=True)
            mm.then_inc(rank_ok, 1)
            pe.wait_ge(route, ROUTE_ALL)

            def expert_of(t):
                return pe.value_load(texp_i[0:1, bass.ds(t, 1)], min_val=0, max_val=E - 1)

            def transpose_x(t, p, g):
                pe.wait_ge(xs_in[p], 16 * g + 16)
                if not (isinstance(t, int) and t < 2):
                    pe.wait_ge(xsT_ok, t - 1)
                for h in range(2):
                    mm = pe.transpose(tr3[0:DH, p, 128 * h:128 * h + 128], xs[p][:, DH * h:DH * h + DH], ident[:, :])
                mm.then_inc(xsT_ps, 1)

            def expert(t, p, g):
                if t_in(t):
                    e = expert_of(t)
                    pe.wait_ge(xsT_ok, t + 1)
                    if not (isinstance(t, int) and t < 2):
                        pe.wait_ge(act_ok, t - 1)
                    for n, w in enumerate((w1_s, w2_s)):
                        for h in range(2):
                            mm = pe.matmul(up_ps[:, p, n, :], xsT[p][:, h, :],
                                           w[:, h, bass.ds(e, 1), :].rearrange("p o h -> p (o h)"),
                                           start=(h == 0), stop=(h == 1))
                    mm.then_inc(up_ok, 1)
                if t_in(t + 2):
                    transpose_x(t + 2, p, g + 1)
                if t_in(t - 1):
                    pe.wait_ge(act_ok, t)
                    if not (isinstance(t, int) and t < 2):
                        pe.wait_ge(actT_ok, t - 1)
                    for c in range(HC):
                        mm = pe.transpose(at_ps[:, 128 * c:128 * c + 128], act_s[1 - p][:, 128 * c:128 * c + 128],
                                          ident[:, :])
                    mm.then_inc(actT_ps, 1)
                if t_in(t - 2):
                    e = expert_of(t - 2)
                    pe.wait_ge(actT_ok, t - 1)
                    if not (isinstance(t, int) and t < 3):
                        pe.wait_ge(ys_ok, t - 2)
                    for c in range(HC):
                        mm = pe.matmul(dn_ps[:, 0:D], actT[p][:, c, :],
                                       w3_s[:, c, bass.ds(e, 1), :].rearrange("p o h -> p (o h)"),
                                       start=(c == 0), stop=(c == HC - 1))
                    mm.then_inc(dn_ok, 1)

            pe.wait_ge(w3_in, 16 * W3_DMAS)
            transpose_x(0, 0, 0)
            transpose_x(1, 1, 0)
            expert_schedule(pe, expert)

        @block.vector
        def _(dve):
            for n, b in enumerate((h0[0], h0[1], xn[0], xn[1])):
                dve.memset(b[:, :, :], 0.0).then_inc(clear1, 1)
            dve.wait_ge(w1_in, 16 * W1_DMAS)
            for t in range(2):
                dve.tensor_tensor(posb[0:ROWS[t], t, :], posb[0:ROWS[t], t, :], emb_bias[0:ROWS[t], t, :], ALU.add)\
                   .then_inc(posb_ok, 1)
            dve.wait_ge(posb_ok, 2)
            dve.wait_ge(clear1, 4)

            def embed(i, p, g):
                dve.wait_ge(emb_mm, i + 1)
                if not (isinstance(i, int) and i < 2):
                    dve.wait_ge(h0_out[p], 16 * g)
                for t in range(2):
                    a = dve.tensor_tensor(h0[p][0:ROWS[t], t, :], emb_ps[0:ROWS[t], p, t, 0:D],
                                          posb[0:ROWS[t], t, :], ALU.add)
                a.then_inc(h0_ok, 1)
                dve.wait_ge(h0_ok, i + 1)
                dve.wait_ge(txt_in[p], 16 * g + 16)
                for t in range(3):
                    dve.bn_stats(bst[p][:, t, :], h0[p][:, t, :]).then_inc(st_chain, 1)
                me, se, mo, so = (bst[p][:, :, c] for c in (1, 2, 4, 5))
                total, diff, sq, mean, var, inv = (sd[p][:, c, :] for c in range(6))
                dve.wait_ge(st_chain, 11 * i + 3)
                dve.tensor_tensor(total, me, mo, ALU.add).then_inc(st_chain, 1)
                dve.tensor_tensor(diff, me, mo, ALU.subtract).then_inc(st_chain, 1)
                dve.tensor_tensor(sq, se, so, ALU.add).then_inc(st_chain, 1)
                dve.wait_ge(st_chain, 11 * i + 6)
                dve.tensor_scalar(mean, total, 0.5, None, ALU.mult).then_inc(st_chain, 1)
                dve.tensor_tensor(diff, diff, diff, ALU.mult).then_inc(st_chain, 1)
                dve.tensor_scalar(var, sq, 1.0 / D, EPS, ALU.mult, ALU.add).then_inc(st_chain, 1)
                dve.wait_ge(st_chain, 11 * i + 9)
                dve.scalar_tensor_tensor(var, diff, 0.25, var, ALU.mult, ALU.add).then_inc(st_chain, 1)
                dve.wait_ge(sqrt_ok, i + 1)
                dve.reciprocal(inv, rt[p][:, :]).then_inc(st_chain, 1)
                dve.wait_ge(st_chain, 11 * i + 11)
                if not (isinstance(i, int) and i < 2):
                    dve.wait_ge(tr_ok, i - 1)
                for t in range(3):
                    a = dve.tensor_scalar(xn[p][:, t, :], h0[p][:, t, :], sd[p][:, 3, t:t + 1], sd[p][:, 5, t:t + 1],
                                          ALU.subtract, ALU.mult)
                a.then_inc(xn_ok, 1)

            embed(0, 0, 0)
            embed(1, 1, 0)
            dve.wait_ge(w2_in, 16 * W2_DMAS)
            dve.wait_ge(set2, 1)
            dve.tensor_scalar(a_neg[:, :, :], a_neg[:, :, :], -1.0, None, ALU.mult).then_inc(set2, 1)
            dve.tensor_tensor(dsum[:, :], dsk[:, 0:J], dsk[:, J:2 * J], ALU.add).then_inc(set2, 1)
            dve.wait_ge(set2, 3)
            dve.wait_ge(gp_set, 2)
            for j in range(J):
                dve.tensor_scalar(diag_d[:, j, :], ident[:, :], dsum[:, j:j + 1], None, ALU.mult).then_inc(set2, 1)
            if B > 2:
                with dve.Fori(1, B // 2) as g:
                    for p in range(2):
                        embed(2 * g + p, p, g)

            dve.wait_ge(pads, 3)

            def conv(i):
                nxt = 0 if i is None else i + 1
                for j in range(J):
                    dve.wait_ge(misc_free, use_count(i, j) + 1)
                    dve.scalar_tensor_tensor(xc[:, j, 1:L], xraw[:, j, 0:L - 1], dww[:, j, 0:1], xc[:, j, 1:L],
                                             ALU.mult, ALU.add).then_inc(xc_left, 1)
                for j in range(J):
                    dve.wait_ge(xc_left, J * nxt + j + 1)
                    dve.scalar_tensor_tensor(xc[:, j, 0:L - 1], xraw[:, j, 1:L], dww[:, j, 2:3], xc[:, j, 0:L - 1],
                                             ALU.mult, ALU.add).then_inc(xc_ok, 1)

            def gate(i, p):
                dve.wait_ge(hc_free, ND * 4 * (i + 1))
                dve.wait_ge(hcg_free, J * 4 * (i + 1))
                if not is_first(i):
                    dve.wait_ge(misc_full, use_count(i, O_LAST) + 1)
                for j in range(J):
                    dve.tensor_tensor(yg[:, j, :], y_ps[:, j, 0:L], z_s[p][:, j, :], ALU.mult).then_inc(gated, 1)

            def body(i, p):
                for unit in range(4):
                    k, U = unit // 2, 4 * i + unit
                    if unit % 2 == 0:
                        dve.wait_ge(du_ok, 2 * i + k + 1)
                    for q in range(1, DP + 1):
                        if not (isinstance(U, int) and U == 0):
                            dve.wait_ge(hc_full, ND * (U - 1) + J * q)
                        dve.wait_ge(bc_full, 2 * DP * U + q)
                        size = J if q < DP else 1
                        for j in range(0, J, size):
                            shape = [128, size, 2, L]
                            dve.tensor_tensor(h_s[:, j:j + size, 2 * q:2 * q + 2, 1:L + 1],
                                              bc_ps[:, (q + 1) % 2, :, 0:L].unsqueeze(1).to_broadcast(shape),
                                              du[p][:, k, j:j + size, :].unsqueeze(2).to_broadcast(shape), ALU.mult)\
                               .then_inc(dbu, size)
                        if unit == 1 and q == 1 and not is_last(i):
                            conv(i)
                    for j in range(J):
                        dve.wait_ge(dbu, ND * U + ND - J + j + 1)
                        dve.wait_ge(dbu_g, J * U + j + 1)
                        dve.wait_ge(da_ok, J * U + j + 1)
                        a = dA[unit % 2][:, j, :, :].rearrange("p n t -> p (n t)")
                        b = h_s[:, j, :, :].rearrange("p n t -> p (n t)")
                        if k == 1:
                            a, b = a[:, ::-1], b[:, ::-1]
                        dve.tensor_tensor_scan(b, a, b, 0.0, ALU.mult, ALU.add).then_inc(scan_ok, 1)
                        if unit == 0 and j == 1 and not is_first(i):
                            gate(i - 1, 1 - p)
                    for q in range(1, DP + 1):
                        dve.wait_ge(bc_full, 2 * DP * U + DP + q)
                        size = J if q == DP else 1
                        for j in range(0, J, size):
                            if q == 1:
                                dve.wait_ge(scan_ok, J * U + j + 1)
                            r = J * (q - 1) + j
                            n = ND * U + r + size - RING
                            if not (isinstance(n, int) and n <= 0):
                                dve.wait_ge(hc_free, n)
                            c = (ND * unit + r) % RING
                            dve.tensor_tensor(hc[:, c:c + size, :, :], h_s[:, j:j + size, 2 * q:2 * q + 2, 1:L + 1],
                                              bc_ps[:, q % 2, :, 0:L].unsqueeze(1).to_broadcast([128, size, 2, L]),
                                              ALU.mult).then_inc(hc_full, size)

            conv(None)
            body(0, 0)
            if B > 2:
                with dve.Fori(0, B // 2 - 1) as g:
                    body(2 * g + 1, 1)
                    body(2 * g + 2, 0)
            body(B - 1, 1)
            gate(B - 1, 1)

            for n, (a, b) in enumerate(H1_PARTS):
                dve.wait_ge(h1_in[n], 16)
                with dve.Fori(a // ROLL, b // ROLL) as g:
                    for r in range(ROLL):
                        t = ROLL * g + r
                        dve.bn_stats(bst2[:, bass.ds(t, 1), :].rearrange("p o s -> p (o s)"),
                                     xn2[:, bass.ds(t, 1), 0:D].rearrange("p o d -> p (o d)")).then_inc(ln2, 1)
            ln2_count = [NT]

            def ln_step(ins):
                ins.then_inc(ln2, 1)
                ln2_count[0] += 1
                dve.wait_ge(ln2, ln2_count[0])

            dve.wait_ge(ln2, NT)
            me, se, mo, so = (bst2[:, :, c] for c in (1, 2, 4, 5))
            ln_step(dve.tensor_tensor(stat[:, 0, :], me, mo, ALU.add))
            ln_step(dve.tensor_tensor(stat[:, 1, :], me, mo, ALU.subtract))
            ln_step(dve.tensor_tensor(stat[:, 2, :], se, so, ALU.add))
            ln_step(dve.tensor_scalar(stat[:, 3, :], stat[:, 0, :], 0.5, None, ALU.mult))
            ln_step(dve.tensor_tensor(stat[:, 1, :], stat[:, 1, :], stat[:, 1, :], ALU.mult))
            ln_step(dve.tensor_scalar(stat[:, 4, :], stat[:, 2, :], 1.0 / D, EPS, ALU.mult, ALU.add))
            ln_step(dve.scalar_tensor_tensor(stat[:, 4, :], stat[:, 1, :], 0.25, stat[:, 4, :], ALU.mult, ALU.add))
            assert ln2_count[0] == LN2_VAR
            dve.wait_ge(sqrt2, 1)
            ln_step(dve.reciprocal(stat[:, 5, :], root[:, :]))
            with dve.Fori(0, NT // ROLL) as g:
                for r in range(ROLL):
                    t = ROLL * g + r
                    x = xn2[:, bass.ds(t, 1), 0:D].rearrange("p o d -> p (o d)")
                    dve.tensor_scalar(x, x, stat[:, 3, bass.ds(t, 1)], stat[:, 5, bass.ds(t, 1)],
                                      ALU.subtract, ALU.mult).then_inc(xn2_ok, 1)

            done = [0]

            def step(ins):
                ins.then_inc(route, 1)
                done[0] += 1
                dve.wait_ge(route, done[0])

            def over_e(x, n=NT):
                return x.unsqueeze(2).to_broadcast([128, n, E])

            dve.wait_ge(lg_ok, NM)
            dve.wait_ge(wr_in, 32)
            for n in range(NB):
                a, b = TB * n, min(TB * n + TB, NT)
                step(dve.tensor_tensor(lg[:, a:b, :], lg_ps[:, n, 0:E * (b - a)].rearrange("p (t e) -> p t e", e=E),
                                       rb_s[:, :].unsqueeze(1).to_broadcast([128, b - a, E]), ALU.add))
            step(dve.tensor_reduce(lmax[:, :], lg[:, :, :], AX.X, ALU.max))
            step(dve.tensor_tensor(lt[:, :, :], lg[:, :, :], over_e(lmax[:, :]), ALU.subtract))
            dve.wait_ge(gp_set, 10)
            step(dve.scalar_tensor_tensor(onehot[:, :, :], lt[:, :, :], 0.0,
                                          prio[:, :].unsqueeze(1).to_broadcast([128, NT, E]), ALU.is_equal, ALU.mult))
            assert done[0] == ROUTE_LT
            step(dve.tensor_reduce(best[:, :], onehot[:, :, :], AX.X, ALU.max))
            step(dve.tensor_tensor(onehot[:, :, :], onehot[:, :, :], over_e(best[:, :]), ALU.is_equal))
            assert done[0] == ROUTE_HOT
            dve.wait_ge(rexp, 1)
            step(dve.tensor_reduce(lmax[:, :], lt[:, :, :], AX.X, ALU.add))
            step(dve.reciprocal(prob[:, :], lmax[:, :]))
            dve.wait_ge(rank_ok, 1)
            for n in range(NB):
                a, b = TB * n, min(TB * n + TB, NT)
                step(dve.tensor_copy(rank_e[:, a:b, :], lg_ps[:, n, 0:E * (b - a)].rearrange("p (t e) -> p t e", e=E)))
                step(dve.tensor_copy(cnt[:, :, a:b],
                                     cnt_ps[n][:, 0:E * (b - a)].rearrange("p (t e) -> p e t", e=E)))
            step(dve.memset(cum[:, :, 0:1], 0.0))
            for e in range(E):
                step(dve.tensor_tensor_scan(cum[:, e, 1:NT + 1], ones[:, 0:NT], cnt[:, e, :], 0.0, ALU.mult, ALU.add))
            step(dve.tensor_scalar(tot_i[:, :], cum[:, :, NT], 127.0, None, ALU.add))
            step(dve.tensor_scalar(tot_i[:, :], tot_i[:, :], -128, None, ALU.bitwise_and))
            step(dve.tensor_copy(pad_f[:, :], tot_i[:, :]))
            step(dve.memset(ends[:, 0:1], 0.0))
            step(dve.tensor_tensor_scan(ends[:, 1:E + 1], ones[:, 0:E], pad_f[:, :], 0.0, ALU.mult, ALU.add))
            step(dve.tensor_tensor(rank_e[:, :, :], rank_e[:, :, :], cum[:, :, 0:NT].rearrange("p e t -> p t e"), ALU.add))
            step(dve.tensor_tensor(rank_e[:, :, :], rank_e[:, :, :],
                                   ends[:, 0:E].unsqueeze(1).to_broadcast([128, NT, E]), ALU.add))
            step(dve.tensor_tensor(rank_e[:, :, :], rank_e[:, :, :], onehot[:, :, :], ALU.mult))
            step(dve.tensor_reduce(slot_f[:, :], rank_e[:, :, :], AX.X, ALU.add))
            step(dve.tensor_copy(slot_u[:, :], slot_f[:, :]))
            step(dve.memset(texp[:, :], 0.0))
            for e in range(1, E):
                step(dve.scalar_tensor_tensor(texp[:, :], start_f[:, :], ends[0:1, e:e + 1], texp[:, :],
                                              ALU.is_ge, ALU.add))
            step(dve.tensor_copy(texp_i[:, :], texp[:, :]))
            assert done[0] == ROUTE_ALL, (done[0], ROUTE_ALL)

            def hold_tokens(t, p, g):
                dve.wait_ge(xs_in[p], 16 * g + 16)
                dve.tensor_copy(hold[p][:, :], xs[p][:, D:D + 1]).then_inc(hold_ok, 1)

            def expert(t, p, g):
                if t_in(t):
                    dve.wait_ge(g1_ok, t + 1)
                    if not (isinstance(t, int) and t < 2):
                        dve.wait_ge(actT_ps, t - 1)
                    dve.tensor_tensor(act_s[p][:, :], g1[p][:, :], up_ps[:, p, 1, :], ALU.mult).then_inc(act_ok, 1)
                if t_in(t - 2):
                    if not (isinstance(t, int) and t < 4):
                        dve.wait_ge(ys_out, 16 * (t - 3))
                    dve.wait_ge(later_ok, t - 1)
                    dve.tensor_copy(tok_u[p][:, :], later[p][:, :]).then_inc(tok_ok, 1)
                    dve.wait_ge(tok_ok, t - 1)
                if t_in(t):
                    dve.wait_ge(hold_ok, t + 1)
                    dve.tensor_copy(later[p][:, :], hold[p][:, :]).then_inc(later_ok, 1)
                    dve.wait_ge(later_ok, t + 1)
                if t_in(t + 2):
                    hold_tokens(t + 2, p, g + 1)
                if t_in(t - 2):
                    dve.wait_ge(dn_ok, t - 1)
                    dve.tensor_copy(ys[p][:, :], dn_ps[:, 0:D]).then_inc(ys_ok, 1)

            hold_tokens(0, 0, 0)
            hold_tokens(1, 1, 0)
            expert_schedule(dve, expert)

            dve.wait_ge(h1_back, 16 * (NT // ROLL))
            for n, a in enumerate(y_parts):
                b = min(a + 8 * ROLL, NT)
                dve.wait_ge(yr_in[n], 16)
                with dve.Fori(a // ROLL, b // ROLL) as g:
                    for r in range(ROLL):
                        t = ROLL * g + r
                        x = xn2[:, bass.ds(t, 1), 0:D].rearrange("p o d -> p (o d)")
                        dve.scalar_tensor_tensor(x, yr[:, bass.ds(t, 1), :].rearrange("p o d -> p (o d)"),
                                                 prob[:, bass.ds(t, 1)], x, ALU.mult, ALU.add).then_inc(fin_ok, 1)


_INS = ["patches", "txt", "convT", "conv_bias", "cls", "pos", "inT", "dw_w", "dw_b", "xpT", "dtT", "dt_b", "a_logs",
        "d_skip", "outT", "router_w", "router_b", "w1", "w2", "w3"]


def kernel(x, txt, L0_tok_conv_w, L0_tok_conv_b, L0_tok_cls_token, L0_tok_pos_emb, L0_attn_in_proj_w, L0_attn_conv_w,
           L0_attn_conv_b, L0_attn_x_proj_w, L0_attn_dt_proj_w, L0_attn_dt_proj_b, L0_attn_A_logs, L0_attn_Ds,
           L0_attn_out_proj_w, L0_ffn_router_w, L0_ffn_router_b, L0_ffn_w1, L0_ffn_w2, L0_ffn_w3):
    import numpy as np
    import concourse.bacc as bacc
    from concourse.bass_utils import run_bass_kernel_spmd

    B, C, H, W = x.shape
    D, _, P, _ = L0_tok_conv_w.shape
    n = H // P
    DH, J = D // 2, L0_attn_out_proj_w.shape[1] // 128
    R = L0_attn_dt_proj_w.shape[2]
    S = L0_attn_A_logs.shape[1]
    E, _, HID = L0_ffn_w1.shape
    f = np.float32
    v = np.asarray(x).reshape(B, C, n, P, n, P).transpose(0, 1, 3, 5, 2, 4).reshape(B, C * P * P // 128, 128, n * n)
    patches = np.zeros((B, 128, C * P * P // 128, n * n + 1), f)
    patches[:, :, :, 1:] = v.transpose(0, 2, 1, 3)
    xw = np.asarray(L0_attn_x_proj_w)
    rows = [xw[k, R:] for k in range(2) for _ in range(3)] + [xw[0, :R], np.zeros((64 - R, xw.shape[2]), f), xw[1, :R]]
    xpT = np.concatenate(rows).T.reshape(J, 128, -1).transpose(1, 0, 2)
    dtw = np.asarray(L0_attn_dt_proj_w)
    dtT = np.concatenate([dtw[0].T, np.zeros((64 - R, J * 128), f), dtw[1].T])

    def by_block(a, *rest):
        return np.asarray(a).reshape(-1, 128, *rest).transpose(1, 0, *range(2, 2 + len(rest)))

    arrays = {
        "patches": patches,
        "txt": np.asarray(txt),
        "convT": np.asarray(L0_tok_conv_w).reshape(D, -1, 128).transpose(2, 1, 0),
        "conv_bias": np.broadcast_to(np.asarray(L0_tok_conv_b), (128, D)),
        "cls": np.asarray(L0_tok_cls_token)[0],
        "pos": np.asarray(L0_tok_pos_emb)[0],
        "inT": np.asarray(L0_attn_in_proj_w).T.reshape(2, DH, -1).transpose(1, 0, 2),
        "dw_w": by_block(L0_attn_conv_w, 3),
        "dw_b": by_block(L0_attn_conv_b),
        "xpT": xpT,
        "dtT": dtT,
        "dt_b": by_block(L0_attn_dt_proj_b),
        "a_logs": by_block(L0_attn_A_logs, S),
        "d_skip": by_block(L0_attn_Ds),
        "outT": by_block(np.asarray(L0_attn_out_proj_w).T, D),
        "router_w": np.asarray(L0_ffn_router_w).reshape(2, DH, E).transpose(1, 0, 2),
        "router_b": np.broadcast_to(np.asarray(L0_ffn_router_b), (128, E)),
        "w1": np.asarray(L0_ffn_w1).reshape(E, 2, DH, HID).transpose(2, 1, 0, 3),
        "w2": np.asarray(L0_ffn_w2).reshape(E, 2, DH, HID).transpose(2, 1, 0, 3),
        "w3": np.asarray(L0_ffn_w3).reshape(E, HID // 128, 128, D).transpose(2, 1, 0, 3),
    }
    nc = bacc.Bacc("TRN2", target_bir_lowering=False, num_devices=1)
    feeds, args = {}, []
    for name in _INS:
        a = np.ascontiguousarray(arrays[name])
        feeds[f"in_{name}"] = a
        args.append(nc.dram_tensor(f"in_{name}", a.shape, mybir.dt.from_np(a.dtype), kind="ExternalInput").ap())
    L = n * n + 1 + txt.shape[1]
    out = nc.dram_tensor("out", (B * L, D), mybir.dt.float32, kind="ExternalOutput").ap()
    early_fusion_kernel(nc, *args, out)
    r = run_bass_kernel_spmd(nc, [feeds], core_ids=[0])
    return r.results[0]["out"].reshape(B, L, D)
```
